# Optimizing a Trainium2 kernel written in Bass

```python
import numpy as np
import jax
import jax.numpy as jnp

def _softmax(x, axis=-1):
    return jax.nn.softmax(x, axis=axis)

def _gelu(x):
    return jax.nn.gelu(x, approximate=True)

def _silu(x):
    return jax.nn.silu(x)

def _sigmoid(x):
    return jax.nn.sigmoid(x)

def _layernorm(x, axis=-1, eps=1e-05):
    m = jnp.mean(x, axis=axis, keepdims=True)
    v = jnp.var(x, axis=axis, keepdims=True)
    return (x - m) / jnp.sqrt(v + eps)

def _scatter_add(tgt, idx, src, axis=0):
    return tgt.at[idx].add(src)

def _segment_sum(src, seg, n):
    return jax.ops.segment_sum(src, seg, n)
kernel_name = 'mk_seq_postln_d1_jaxref_r8_c03fac'

def setup_inputs(seed: int=0):
    np.random.seed(seed)
    _w = jnp.asarray

    def _L0_attn_setup():
        import jax, jax.numpy as jnp
        import numpy as np
        HEADS = 4
        EPS = 1e-05
        GATE_LOGIT_NORMALIZER = 16.0
        B, N, D = (4, 256, 128)
        DK, DV, R = (128, 256, 16)

        def _gla_scan(q, k, v, gk):
            dk, dv = (q.shape[1], v.shape[1])

            def step(S, inp):
                q_t, k_t, v_t, g_t = inp
                S = S * jnp.exp(g_t)[:, None] + k_t[:, None] * v_t[None, :]
                return (S, q_t @ S)
            S0 = jnp.zeros((dk, dv), q.dtype)
            _, o = jax.lax.scan(step, S0, (q, k, v, gk))
            return o
        key = jax.random.key(seed)
        ks = jax.random.split(key, 10)
        s = 0.02
        return {'x': jax.random.normal(ks[0], (B, N, D), jnp.float32), 'Wq': jax.random.normal(ks[1], (D, DK), jnp.float32) * s, 'Wk': jax.random.normal(ks[2], (D, DK), jnp.float32) * s, 'Wv': jax.random.normal(ks[3], (D, DV), jnp.float32) * s, 'Wg': jax.random.normal(ks[4], (D, DV), jnp.float32) * s, 'Wgk1': jax.random.normal(ks[5], (D, R), jnp.float32) * s, 'Wgk2': jax.random.normal(ks[6], (R, DK), jnp.float32) * s, 'bgk2': jnp.zeros((DK,), jnp.float32), 'Wo': jax.random.normal(ks[7], (DV, D), jnp.float32) * s, 'g_norm_weight': jnp.ones((DV // HEADS,), jnp.float32)}
    _L0_attn_in = _L0_attn_setup()

    def _L0_ffn_setup():
        import jax, jax.numpy as jnp
        import numpy as np
        K = 2
        key = jax.random.key(seed)
        ks = jax.random.split(key, 7)
        B, S, D, E = (2, 256, 128, 8)
        H = 4 * D
        sd = 1.0 / np.sqrt(D)
        sh = 1.0 / np.sqrt(H)
        return {'x': jax.random.normal(ks[0], (B, S, D), jnp.float32), 'Wr': jax.random.normal(ks[1], (D, E), jnp.float32) * sd, 'br': jax.random.normal(ks[2], (E,), jnp.float32) * sd, 'W1': jax.random.normal(ks[3], (E, D, H), jnp.float32) * sd, 'b1': jax.random.normal(ks[4], (E, H), jnp.float32) * sd, 'W2': jax.random.normal(ks[5], (E, H, D), jnp.float32) * sh, 'b2': jax.random.normal(ks[6], (E, D), jnp.float32) * sh}
    _L0_ffn_in = _L0_ffn_setup()
    _d = {'L0_attn_x': _L0_attn_in['x'], 'L0_attn_Wq': _L0_attn_in['Wq'], 'L0_attn_Wk': _L0_attn_in['Wk'], 'L0_attn_Wv': _L0_attn_in['Wv'], 'L0_attn_Wg': _L0_attn_in['Wg'], 'L0_attn_Wgk1': _L0_attn_in['Wgk1'], 'L0_attn_Wgk2': _L0_attn_in['Wgk2'], 'L0_attn_bgk2': _L0_attn_in['bgk2'], 'L0_attn_Wo': _L0_attn_in['Wo'], 'L0_attn_g_norm_weight': _L0_attn_in['g_norm_weight'], 'L0_ffn_Wr': _L0_ffn_in['Wr'], 'L0_ffn_br': _L0_ffn_in['br'], 'L0_ffn_W1': _L0_ffn_in['W1'], 'L0_ffn_b1': _L0_ffn_in['b1'], 'L0_ffn_W2': _L0_ffn_in['W2'], 'L0_ffn_b2': _L0_ffn_in['b2']}
    _x0 = _d['L0_attn_x']
    _d['L0_attn_x'] = jax.random.normal(jax.random.fold_in(jax.random.key(seed), 1), (1, 2048, 128), dtype=_x0.dtype)
    del _x0
    return _d

def reference(L0_attn_x, L0_attn_Wq, L0_attn_Wk, L0_attn_Wv, L0_attn_Wg, L0_attn_Wgk1, L0_attn_Wgk2, L0_attn_bgk2, L0_attn_Wo, L0_attn_g_norm_weight, L0_ffn_Wr, L0_ffn_br, L0_ffn_W1, L0_ffn_b1, L0_ffn_W2, L0_ffn_b2):

    def _L0_attn_ref(x, Wq, Wk, Wv, Wg, Wgk1, Wgk2, bgk2, Wo, g_norm_weight):
        import jax, jax.numpy as jnp
        import numpy as np
        HEADS = 4
        EPS = 1e-05
        GATE_LOGIT_NORMALIZER = 16.0
        B, N, D = (4, 256, 128)
        DK, DV, R = (128, 256, 16)

        def _gla_scan(q, k, v, gk):
            dk, dv = (q.shape[1], v.shape[1])

            def step(S, inp):
                q_t, k_t, v_t, g_t = inp
                S = S * jnp.exp(g_t)[:, None] + k_t[:, None] * v_t[None, :]
                return (S, q_t @ S)
            S0 = jnp.zeros((dk, dv), q.dtype)
            _, o = jax.lax.scan(step, S0, (q, k, v, gk))
            return o
        b, n, d = x.shape
        h = HEADS
        dk = Wq.shape[1] // h
        dv = Wv.shape[1] // h
        split = lambda t, hd: t.reshape(b, n, h, hd).transpose(0, 2, 1, 3)
        q = split(x @ Wq, dk) * dk ** (-0.5)
        k = split(x @ Wk, dk)
        v = split(x @ Wv, dv)
        gk = jax.nn.log_sigmoid(x @ Wgk1 @ Wgk2 + bgk2) / GATE_LOGIT_NORMALIZER
        gk = split(gk, dk)
        o = jax.vmap(jax.vmap(_gla_scan))(q, k, v, gk)
        o = o.transpose(0, 2, 1, 3)
        g = (x @ Wg).reshape(b, n, h, dv)
        o = o * jax.lax.rsqrt(jnp.mean(o * o, axis=-1, keepdims=True) + EPS) * g_norm_weight
        o = o * (g * jax.nn.sigmoid(g))
        return o.reshape(b, n, h * dv) @ Wo

    def _L0_ffn_ref(x, Wr, br, W1, b1, W2, b2):
        import jax, jax.numpy as jnp
        import numpy as np
        K = 2
        E = Wr.shape[-1]
        scores = jnp.einsum('bsd,de->bse', x, Wr) + br
        _, topk_idx = jax.lax.top_k(scores, K)
        indicator = jax.nn.one_hot(topk_idx, E, dtype=scores.dtype).sum(-2)
        neg_inf = jnp.asarray(-jnp.inf, scores.dtype)
        weights = jax.nn.softmax(jnp.where(indicator > 0, scores, neg_inf), axis=-1)
        out = jnp.zeros_like(x)
        for i in range(E):
            xi = x * indicator[..., i:i + 1]
            h = jax.nn.relu(jnp.einsum('bsd,dh->bsh', xi, W1[i]) + b1[i])
            yi = jnp.einsum('bsh,hd->bsd', h, W2[i]) + b2[i]
            out = out + yi * weights[..., i:i + 1]
        return out
    x = L0_attn_x
    x = _layernorm(x + _L0_attn_ref(x, L0_attn_Wq, L0_attn_Wk, L0_attn_Wv, L0_attn_Wg, L0_attn_Wgk1, L0_attn_Wgk2, L0_attn_bgk2, L0_attn_Wo, L0_attn_g_norm_weight), axis=-1)
    x = _layernorm(x + _L0_ffn_ref(x, L0_ffn_Wr, L0_ffn_br, L0_ffn_W1, L0_ffn_b1, L0_ffn_W2, L0_ffn_b2), axis=-1)
    return x

_drawn_inputs = setup_inputs


def setup_inputs(seed=0):
    import zlib

    import numpy as np

    out = dict(_drawn_inputs(seed))
    spreads = {'L0_attn_bgk2': (0.0, 2.0), 'L0_attn_g_norm_weight': (1.0, 0.556)}
    factors = {'L0_attn_Wgk1': 27.575, 'L0_attn_Wgk2': 23.258}
    for name, (base, spread) in spreads.items():
        noise = np.random.default_rng([zlib.crc32(name.encode()), seed]).standard_normal(out[name].shape)
        drawn = base * np.exp(spread * noise) if base else spread * noise
        out[name] = jnp.asarray(drawn.astype(out[name].dtype))
    for name, factor in factors.items():
        out[name] = (out[name] * factor).astype(out[name].dtype)
    return out
```

```python
from contextlib import ExitStack

import concourse.bass as bass
from concourse import mybir

F32 = mybir.dt.float32
ACT = mybir.ActivationFunctionType
ALU = mybir.AluOpType
AX_X = mybir.AxisListType.X

P = 128
HEADS = 4
EPS = 1e-5
GATE_NORMALIZER = 16.0
GROUP = 512
SUB = 64
SAFE = 40.0
BIG = 3.0e38


def build(nc, x, Wq, Wk, Wv, Wg, Wgk1, Wgk2, bgk2, Wo, g_norm, Wr, br, W1, b1, W2, b2, out):
    _, N, D = x.shape
    R = Wgk1.shape[1]
    DV = Wv.shape[1]
    E = Wr.shape[1]
    H = W1.shape[2]
    dk = P // HEADS
    dv = DV // HEADS
    T = N // P
    NG = N // GROUP
    TG = GROUP // P
    SG_ = GROUP // SUB
    NS = N // SUB
    HC = H // P
    DVC = DV // P
    assert D == P and Wq.shape[1] == P and T % 2 == 0

    x_tok = x.rearrange("a (t p) d -> p (a t) d", p=P)
    out_tok = out.rearrange("a (t p) d -> p (a t) d", p=P)

    with ExitStack() as ctx:
        def sb(name, shape, dt=F32):
            return ctx.enter_context(nc.sbuf_tensor(name, shape, dt))

        def sem(name):
            return ctx.enter_context(nc.semaphore(name))

        x_sb = sb("x_sb", [P, T, D])
        wq_sb = sb("wq_sb", [P, P])
        wk_sb = sb("wk_sb", [P, P])
        wv_sb = sb("wv_sb", [P, DV])
        wg_sb = sb("wg_sb", [P, DV])
        wgk1_sb = sb("wgk1_sb", [P, R])
        wgk2_sb = sb("wgk2_sb", [R, P])
        bgk2_sb = sb("bgk2_sb", [P, 1])
        wo_in = sb("wo_in", [P, DVC, D])
        gnorm_sb = sb("gnorm_sb", [P, 1])
        wr_sb = sb("wr_sb", [P, E])
        br_sb = sb("br_sb", [P, E])
        w1_sb = sb("w1_sb", [P, E, H])
        b1_in = sb("b1_in", [E * HC, P])
        b1_sb = sb("b1_sb", [P, E, HC])
        w2_sb = sb("w2_sb", [P, E, HC, D])
        b2_sb = sb("b2_sb", [E, D])
        ident = sb("ident", [P, P])
        causal = sb("causal", [P, P])
        head_mask = sb("head_mask", [P, HEADS, dv])
        seg = sb("seg", [P, GROUP])
        rank_e = sb("rank_e", [P, E])
        xT = sb("xT", [P, N])
        wgk1T = sb("wgk1T", [R, P])
        wgk = sb("wgk", [P, P])
        wo_sb = sb("wo_sb", [P, DVC, D])
        qT = sb("qT", [P, N])
        kT = sb("kT", [P, N])
        zb = sb("zb", [P, GROUP])
        soft = sb("soft", [P, GROUP])
        gT = sb("gT", [P, N])
        cum = sb("cum", [P, N])
        dist = sb("dist", [P, GROUP])
        em = sb("em", [P, NS])
        er = sb("er", [P, NS])
        rest = sb("rest", [P, NS])
        et = sb("et", [P, NS])
        scq = sb("scq", [P, NS])
        sck = sb("sck", [P, NS])
        tile_decay = sb("tile_decay", [P, T])
        eq = sb("eq", [P, GROUP])
        ek = sb("ek", [P, GROUP])
        qm = sb("qm", [P, N])
        km = sb("km", [P, N])
        qc = sb("qc", [P, N])
        kc = sb("kc", [P, N])
        qx = sb("qx", [P, T, SUB])
        kx = sb("kx", [P, T, SUB])
        v_sb = sb("v_sb", [P, T, DV])
        gate = sb("gate", [P, T, DV])
        aT = sb("aT", [P, 2, HEADS, P])
        kcT = sb("kcT", [P, 2, P])
        state = sb("state", [P, 2, dv])
        state_bd = sb("state_bd", [P, 2, HEADS, dv])
        sq = sb("sq", [P, DV])
        ms = sb("ms", [P, 2, HEADS])
        rms = sb("rms", [P, 2, HEADS])
        rrms = sb("rrms", [P, 2, HEADS])
        og = sb("og", [P, 2, DV])
        oT = sb("oT", [P, 2, DVC, P])
        res = sb("res", [P, 2, D])
        stats = sb("stats", [P, 2, 6])
        mv = sb("mv", [P, 2, 2])
        std = sb("std", [P, 2, 1])
        rstd = sb("rstd", [P, 2, 1])
        x1 = sb("x1", [P, T, D])
        x1T = xT
        score = sb("score", [P, T, E])
        hit = sb("hit", [P, T, E])
        pri = sb("pri", [P, T, E])
        first = sb("first", [P, T, E])
        second = sb("second", [P, T, E])
        score2 = sb("score2", [P, T, E])
        top1 = sb("top1", [P, T])
        top2 = sb("top2", [P, T])
        best = sb("best", [P, T])
        gap = sb("gap", [P, T])
        egap = sb("egap", [P, T])
        wsum = sb("wsum", [P, T])
        wt1 = sb("wt1", [P, T])
        wt2 = sb("wt2", [P, T])
        weight = sb("weight", [P, T, E])
        weightT = kT[0:E, :]
        span = sb("span", [P, 2, NS])
        widest = sb("widest", [P, 1])
        worst = sb("worst", [1, 1])
        wide_flag = sb("wide_flag", [1, 1], mybir.dt.int32)
        decay, outer, states = qm, km, kc
        q_states = qc
        v_col = x1[:, :, :].rearrange("p t (h k) -> p t h k", k=dk)
        assert 2 * HC * GROUP == T * DV and 2 * T * D == T * DV
        hT = gate[:, :, :].rearrange("p t v -> p (t v)").rearrange("p (b j c) -> p b j c", b=2, j=HC)
        acc = v_sb[:, 0:T // 2, :].rearrange("p t v -> p (t v)").rearrange("p (t d) -> p t d", d=D)
        result = v_sb[:, T // 2:T, :].rearrange("p t v -> p (t v)").rearrange("p (t d) -> p t d", d=D)
        fstats = sb("fstats", [P, T, 6])
        fmv = sb("fmv", [P, T, 2])
        fstd = sb("fstd", [P, T, 1])
        frstd = sb("frstd", [P, T, 1])

        bank = [ctx.enter_context(nc.psum_tensor(f"bank{i}", [P, 512], F32)) for i in range(8)]

        s_x = [sem(f"x_loaded{g}") for g in range(NG)]
        s_gatew = sem("gate_weights_loaded")
        s_projw = sem("projection_weights_loaded")
        s_vgw = sem("value_weights_loaded")
        s_wo = sem("wo_loaded")
        s_router = sem("router_loaded")
        s_b1 = sem("b1_loaded")
        s_ffn1 = sem("w1_loaded")
        s_ffn2 = sem("w2_loaded")
        s_stored = sem("stored")
        s_const = sem("constants_made")
        s_seed = sem("constants_zeroed")
        s_dinit = sem("vector_buffers_set")
        s_span0 = sem("decay_spans_done")
        s_widest = sem("widest_span_of_channels")
        s_spanT = sem("widest_spans_transposed")
        s_worst = sem("widest_span_of_all")
        s_flag = sem("range_flag_ready")
        s_turn = sem("general_path_turn")
        s_pause = sem("general_path_pause")
        s_job = sem("projection_in_psum")
        s_jact = sem("act_emptied_bank")
        s_jdve = sem("dve_emptied_bank")
        s_wo2 = sem("wo_scaled")
        s_abs = sem("abs_done")
        s_exp = sem("exp_done")
        s_soft = sem("softplus_done")
        s_g = sem("gate_log_done")
        s_cum = sem("cumsum_done")
        s_dist0 = sem("distance_done")
        s_rest = sem("rest_done")
        s_dist = sem("distance_clamped")
        s_eq = sem("decay_factors_done")
        s_small = sem("block_factors_done")
        s_scq = sem("block_scales_done")
        s_qm = sem("qm_done")
        s_qc = sem("q_factors_done")
        s_km = sem("km_done")
        s_kc = sem("k_factors_done")
        s_a = sem("scores_in_psum")
        s_aT = sem("scores_masked")
        s_kt = sem("kc_transposed")
        s_kcT = sem("kc_copied")
        s_kv = sem("state_update_in_psum")
        s_state = sem("state_updated")
        s_bd = sem("state_expanded")
        s_o = sem("o_in_psum")
        s_sq = sem("o_squared")
        s_ms0 = sem("square_sum_done")
        s_ms = sem("mean_square_done")
        s_rms = sem("rms_done")
        s_rr = sem("rrms_done")
        s_og = sem("o_gated")
        s_ot = sem("o_transposed")
        s_oT = sem("oT_copied")
        s_y = sem("attention_in_psum")
        s_res = sem("residual_done")
        s_st = sem("stats_done")
        s_mv = sem("mean_var_done")
        s_veps = sem("var_eps_done")
        s_std = sem("std_done")
        s_rstd = sem("rstd_done")
        s_x1 = sem("x1_done")
        s_xt = sem("x1_transposed")
        s_x1T = sem("x1T_copied")
        s_sc = sem("scores_routed")
        s_route = sem("routing_step")
        s_route_in = sem("score_kept")
        s_egap = sem("exp_gap_done")
        s_weight = sem("weights_done")
        s_wt = sem("weights_transposed")
        s_wT = sem("weightT_copied")
        s_bias = sem("expert_bias_in_psum")
        s_acc0 = sem("acc_started")
        s_h = sem("hidden_in_psum")
        s_ha = sem("hidden_copied_by_act")
        s_hd = sem("hidden_copied_by_dve")
        s_ye = sem("expert_out_in_psum")
        s_acc = sem("acc_added")
        s_fst = sem("final_stats")
        s_fmv = sem("final_mean_var")
        s_fve = sem("final_var_eps")
        s_fstd = sem("final_std")
        s_frs = sem("final_rstd")
        s_res2 = sem("result_done")

        jobs = []
        for g in range(NG):
            jobs.append(("xT", g, "dve"))
            if g == 0:
                jobs += [("wgk1T", 0, "dve"), ("wgk", 0, "dve")]
            jobs += [("z", g, "dve"), ("q", g, "act"), ("k", g, "act")]
        jobs.append(("b1T", 0, "dve"))
        jobs.append(("span", 0, "dve"))
        for g in range(2 * NG):
            jobs += [("v", g, "dve"), ("g", g, "act")]
        at = {job[:2]: i for i, job in enumerate(jobs)}

        def emptied(i):
            engine = jobs[i][2]
            return (s_jact if engine == "act" else s_jdve), sum(j[2] == engine for j in jobs[:i + 1])

        def bank_of(kind, g):
            return bank[at[kind, g] % 8]

        n_act = sum(j[2] == "act" for j in jobs)
        n_dve = len(jobs) - n_act

        def sub3(ap, n):
            return ap.rearrange("p (n c) -> p n c", c=n)

        def wide(ap, n):
            return ap.unsqueeze(2).to_broadcast([ap.shape[0], ap.shape[1], n])

        FFN = [(e, g) for e in range(E) for g in range(NG)]

        V_STEPS = 5 + 2 * NG
        T_STEPS = 25
        V_BASE = 1
        T_BASE = V_BASE + dv * V_STEPS
        v_heads = v_sb[:, :, :].rearrange("p t (h v) -> p t h v", v=dv)
        head_pick = head_mask[:, :, 0]

        block = ctx.enter_context(nc.Block())

        @block.sync
        def _(sp):
            for g in range(NG):
                sp.dma_start(x_sb[:, g * TG:(g + 1) * TG, :], x_tok[:, g * TG:(g + 1) * TG, :]).then_inc(s_x[g], 16)
            sp.dma_start(wv_sb[:, :], Wv).then_inc(s_vgw, 16)
            sp.dma_start(wg_sb[:, :], Wg).then_inc(s_vgw, 16)
            sp.dma_start(wo_in[:, :, :], Wo.rearrange("(c p) d -> p c d", p=P)).then_inc(s_wo, 16)
            for c in range(DVC * P // dv // DVC):
                sp.dma_start(gnorm_sb[c * dv:(c + 1) * dv, :], g_norm.rearrange("(p a) -> p a", a=1)).then_inc(s_wo, 16)
            sp.dma_start(w1_sb[:, :, :], W1.rearrange("e p h -> p e h")).then_inc(s_ffn1, 16)
            sp.dma_start(w2_sb[:, :, :, :], W2.rearrange("e (j p) d -> p e j d", p=P)).then_inc(s_ffn2, 16)
            for g in range(NG):
                sp.wait_ge(s_res2, (g + 1) * TG)
                sp.dma_start(out_tok[:, g * TG:(g + 1) * TG, :], result[:, g * TG:(g + 1) * TG, :]).then_inc(s_stored, 16)
            sp.wait_ge(s_stored, 16 * NG)

        @block.gpsimd
        def _(pool):
            pool.memset(ident[:, :], 0.0).then_inc(s_seed, 1)
            pool.memset(causal[:, :], 1.0).then_inc(s_seed, 1)
            pool.memset(head_mask[:, :, :], 0.0).then_inc(s_seed, 1)
            pool.wait_ge(s_seed, 3)
            pool.affine_select(out=ident[:, :], in_=ident[:, :], compare_op=ALU.not_equal, fill=1.0,
                               base=0, pattern=[[-1, P]], channel_multiplier=1).then_inc(s_const, 1)
            pool.affine_select(out=causal[:, :], in_=causal[:, :], compare_op=ALU.is_ge, fill=0.0,
                               base=0, pattern=[[1, P]], channel_multiplier=-1).then_inc(s_const, 1)
            for h in range(HEADS):
                pool.wait_ge(s_const, 2 + h)
                pool.memset(head_mask[h * dk:(h + 1) * dk, h, :], 1.0).then_inc(s_const, 1)
            pool.wait_ge(s_const, 2 + HEADS)
            pool.iota(rank_e[:, :], pattern=[[-1, E]], base=E, channel_multiplier=0,
                      allow_small_or_imprecise_dtypes=True).then_inc(s_const, 1)
            for g in range(NG):
                c = slice(g * GROUP, (g + 1) * GROUP)
                n = slice(g * SG_, (g + 1) * SG_)
                pool.wait_ge(s_eq, 2 * (g + 1))
                pool.wait_ge(s_jact, emptied(at["k", g])[1])
                pool.tensor_tensor(km[:, c], kT[:, c], ek[:, :], ALU.mult).then_inc(s_km, 1)
                pool.wait_ge(s_km, g + 1)
                pool.wait_ge(s_scq, 4 * (g + 1))
                pool.tensor_tensor(sub3(kc[:, c], SUB), sub3(km[:, c], SUB), wide(sck[:, n], SUB), ALU.mult).then_inc(s_kc, 1)
                pool.wait_ge(s_small, 3 * (g + 1))
                pool.tensor_tensor(kx[:, g * TG:(g + 1) * TG, :], sub3(km[:, c], SUB)[:, 0::2, :],
                                   wide(er[:, n][:, 0::2], SUB), ALU.mult).then_inc(s_kc, 1)
            for t in range(1, T):
                pool.wait_ge(s_state, t)
                if t >= 3:
                    pool.wait_ge(s_o, t - 2)
                pool.tensor_tensor(state_bd[:, t % 2, :, :],
                                   state[:, (t - 1) % 2, :].unsqueeze(1).to_broadcast([P, HEADS, dv]),
                                   head_mask[:, :, :], ALU.mult).then_inc(s_bd, 1)

        @block.scalar
        def _(act):
            act.dma_start(wgk1_sb[:, :], Wgk1).then_inc(s_gatew, 16)
            act.dma_start(wgk2_sb[:, :], Wgk2).then_inc(s_gatew, 16)
            act.dma_start(bgk2_sb[:, :], bgk2.rearrange("(p a) -> p a", a=1)).then_inc(s_gatew, 16)
            act.dma_start(wq_sb[:, :], Wq).then_inc(s_projw, 16)
            act.dma_start(wk_sb[:, :], Wk).then_inc(s_projw, 16)
            act.dma_start(wr_sb[:, :], Wr).then_inc(s_router, 16)
            act.dma_start(br_sb[:, :], br.partition_broadcast(P)).then_inc(s_router, 16)
            act.dma_start(b2_sb[:, :], b2).then_inc(s_router, 16)
            act.dma_start(b1_in[:, :], b1.rearrange("e (j p) -> (e j) p", p=P)).then_inc(s_b1, 16)
            act.preload_act_table_set("natural_log_exp_and_others")
            for g in range(NG):
                c = slice(g * GROUP, (g + 1) * GROUP)
                n = slice(g * SG_, (g + 1) * SG_)
                act.wait_ge(s_jdve, emptied(at["z", g])[1])
                if g:
                    act.wait_ge(s_g, g)
                act.activation(soft[:, :], zb[:, :], ACT.Abs).then_inc(s_abs, 1)
                act.wait_ge(s_abs, g + 1)
                act.activation(soft[:, :], soft[:, :], ACT.Exp, scale=-1.0).then_inc(s_exp, 1)
                act.wait_ge(s_exp, g + 1)
                act.activation(soft[:, :], soft[:, :], ACT.Ln, bias=1.0).then_inc(s_soft, 1)
                act.wait_ge(s_job, at["q", g] + 1)
                act.activation(qT[:, c], bank_of("q", g)[:, :], ACT.Copy, scale=float(dk) ** -0.5).then_inc(s_jact, 1)
                act.wait_ge(s_job, at["k", g] + 1)
                act.activation(kT[:, c], bank_of("k", g)[:, :], ACT.Copy).then_inc(s_jact, 1)
                act.wait_ge(s_cum, g + 1)
                act.wait_ge(s_rest, g + 1)
                cg = sub3(cum[:, c], SUB)
                act.activation(em[:, n], cg[:, :, SUB // 2 - 1], ACT.Exp, scale=1 / GATE_NORMALIZER).then_inc(s_small, 1)
                act.activation(er[:, n], rest[:, n], ACT.Exp, scale=1 / GATE_NORMALIZER).then_inc(s_small, 1)
                act.activation(et[:, n], cg[:, :, SUB - 1], ACT.Exp, scale=1 / GATE_NORMALIZER).then_inc(s_small, 1)
                act.wait_ge(s_dist, g + 1)
                if g:
                    act.wait_ge(s_qm, g)
                    act.wait_ge(s_km, g)
                act.activation(eq[:, :], dist[:, :], ACT.Exp, scale=1 / GATE_NORMALIZER).then_inc(s_eq, 1)
                act.activation(ek[:, :], dist[:, :], ACT.Exp, scale=-1 / GATE_NORMALIZER).then_inc(s_eq, 1)
            for g in range(2 * NG):
                act.wait_ge(s_job, at["g", g] + 1)
                act.activation(gate[:, 2 * g:2 * g + 2, :], bank_of("g", g)[:, :].rearrange("p (t v) -> p t v", v=DV),
                               ACT.Silu).then_inc(s_jact, 1)

            def copy_kcT(t):
                act.wait_ge(s_kt, t + 1)
                if t >= 2:
                    act.wait_ge(s_kv, t - 1)
                act.activation(kcT[:, t % 2, :], bank[6][:, 0:P], ACT.Copy).then_inc(s_kcT, 1)

            def square_o(t):
                act.wait_ge(s_o, t + 1)
                if t >= 1:
                    act.wait_ge(s_ms0, t)
                act.activation(sq[:, :], bank[4 + t % 2][:, 0:DV], ACT.Square).then_inc(s_sq, 1)

            def root(t):
                act.wait_ge(s_ms, t + 1)
                act.activation(rms[:, t % 2, :], ms[:, t % 2, :], ACT.Sqrt).then_inc(s_rms, 1)

            def copy_oT(t):
                act.wait_ge(s_ot, t + 1)
                if t >= 2:
                    act.wait_ge(s_y, t - 1)
                act.activation(oT[:, t % 2, :, :], bank[6][:, 0:DV].rearrange("p (c t) -> p c t", t=P),
                               ACT.Copy).then_inc(s_oT, 1)

            def std_of(t):
                act.wait_ge(s_veps, t + 1)
                act.activation(std[:, t % 2, :], mv[:, t % 2, 1:2], ACT.Sqrt).then_inc(s_std, 1)

            for i in range(T + 4):
                if i < T:
                    copy_kcT(i)
                if 0 <= i - 1 < T:
                    square_o(i - 1)
                    root(i - 1)
                if 0 <= i - 2 < T:
                    copy_oT(i - 2)
                if 0 <= i - 3 < T:
                    std_of(i - 3)
            act.wait_ge(s_flag, 1)
            too_wide = act.value_load(wide_flag[0:1, 0:1], min_val=0, max_val=1)
            with act.If(too_wide):
                act.wait_ge(s_route_in, T)
                act.activation(decay[:, :], gT[:, :], ACT.Exp, scale=1 / GATE_NORMALIZER).then_inc(s_turn, 1)
                with act.Fori(0, T) as t:
                    turn = t * T_STEPS + T_BASE
                    act.wait_ge(s_turn, turn)
                    act.activation(sq[:, :], v_sb[:, bass.ds(t, 1), :].rearrange("p a v -> p (a v)"), ACT.Square).then_inc(s_turn, 1)
                    act.wait_ge(s_turn, turn + 3)
                    act.activation(rms[:, 0, :], ms[:, 0, :], ACT.Sqrt).then_inc(s_turn, 1)
                    act.wait_ge(s_turn, turn + 10)
                    act.activation(oT[:, 0, :, :], bank[6][:, 0:DV].rearrange("p (c t) -> p c t", t=P), ACT.Copy).then_inc(s_turn, 1)
                    act.wait_ge(s_turn, turn + 16)
                    act.activation(std[:, 0, :], mv[:, 0, 1:2], ACT.Sqrt).then_inc(s_turn, 1)
            act.wait_ge(s_route, 12)
            act.activation(egap[:, :], gap[:, :], ACT.Exp).then_inc(s_egap, 1)
            for k, (e, g) in enumerate(FFN):
                for j in range(0, HC, 2):
                    act.wait_ge(s_h, k * HC + j + 1)
                    if k >= 2:
                        act.wait_ge(s_ye, (k - 1) * TG)
                    act.activation(hT[:, k % 2, j, :], bank[j][:, :], ACT.Relu, bias=b1_sb[:, e, j:j + 1]).then_inc(s_ha, 1)
            for t in range(T):
                act.wait_ge(s_fve, t + 1)
                act.activation(fstd[:, t, :], fmv[:, t, 1:2], ACT.Sqrt).then_inc(s_fstd, 1)

        @block.vector
        def _(dve):
            dve.memset(seg[:, :], 1.0).then_inc(s_dinit, 1)
            dve.memset(aT[:, :, :, :], 0.0).then_inc(s_dinit, 1)
            dve.wait_ge(s_dinit, 2)
            dve.memset(seg[:, 0::SUB], 0.0).then_inc(s_dinit, 1)

            def empty(kind, g, dst):
                dve.wait_ge(s_job, at[kind, g] + 1)
                rows, cols = dst.shape[0], 1
                return dst, bank_of(kind, g)

            for g in range(NG):
                c = slice(g * GROUP, (g + 1) * GROUP)
                n = slice(g * SG_, (g + 1) * SG_)
                dve.wait_ge(s_job, at["xT", g] + 1)
                dve.tensor_copy(xT[:, c], bank_of("xT", g)[:, :]).then_inc(s_jdve, 1)
                if g == 0:
                    dve.wait_ge(s_job, at["wgk1T", 0] + 1)
                    dve.tensor_copy(wgk1T[:, :], bank_of("wgk1T", 0)[0:R, 0:P]).then_inc(s_jdve, 1)
                    dve.wait_ge(s_job, at["wgk", 0] + 1)
                    dve.tensor_copy(wgk[:, :], bank_of("wgk", 0)[:, 0:P]).then_inc(s_jdve, 1)
                dve.wait_ge(s_job, at["z", g] + 1)
                if g:
                    dve.wait_ge(s_abs, g)
                    dve.wait_ge(s_g, g)
                dve.tensor_scalar(zb[:, :], bank_of("z", g)[:, :], bgk2_sb[:, 0:1], None, ALU.add).then_inc(s_jdve, 1)
                dve.wait_ge(s_soft, g + 1)
                dve.wait_ge(s_jdve, emptied(at["z", g])[1])
                dve.scalar_tensor_tensor(gT[:, c], zb[:, :], 0.0, soft[:, :], ALU.min, ALU.subtract).then_inc(s_g, 1)
                dve.wait_ge(s_g, g + 1)
                dve.wait_ge(s_dinit, 3)
                dve.tensor_tensor_scan(cum[:, c], seg[:, :], gT[:, c], 0.0, ALU.mult, ALU.add).then_inc(s_cum, 1)
                dve.wait_ge(s_cum, g + 1)
                cg = sub3(cum[:, c], SUB)
                dve.tensor_tensor(rest[:, n], cg[:, :, SUB - 1], cg[:, :, SUB // 2 - 1], ALU.subtract).then_inc(s_rest, 1)
                dve.tensor_tensor(span[:, 0, n], cg[:, :, 0], cg[:, :, SUB // 2 - 1], ALU.subtract).then_inc(s_span0, 1)
                dve.tensor_tensor(span[:, 1, n], cg[:, :, SUB // 2 - 1], cg[:, :, SUB - 1], ALU.subtract).then_inc(s_span0, 1)
                if g:
                    dve.wait_ge(s_eq, 2 * g)
                dve.tensor_tensor(sub3(dist[:, :], SUB), cg, wide(cg[:, :, SUB // 2 - 1], SUB), ALU.subtract).then_inc(s_dist0, 1)
                dve.wait_ge(s_dist0, g + 1)
                dve.tensor_scalar(dist[:, :], dist[:, :], SAFE * GATE_NORMALIZER, -SAFE * GATE_NORMALIZER,
                                  ALU.min, ALU.max).then_inc(s_dist, 1)
                dve.wait_ge(s_small, 3 * (g + 1))
                pair = lambda a: a[:, n].rearrange("p (t two) -> p t two", two=2)
                dve.tensor_copy(pair(scq)[:, :, 0], pair(em)[:, :, 0]).then_inc(s_scq, 1)
                dve.tensor_tensor(pair(scq)[:, :, 1], pair(em)[:, :, 1], pair(et)[:, :, 0], ALU.mult).then_inc(s_scq, 1)
                dve.tensor_copy(pair(sck)[:, :, 1], pair(er)[:, :, 1]).then_inc(s_scq, 1)
                dve.tensor_tensor(pair(sck)[:, :, 0], pair(er)[:, :, 0], pair(et)[:, :, 1], ALU.mult).then_inc(s_scq, 1)
                dve.tensor_tensor(tile_decay[:, g * TG:(g + 1) * TG], pair(et)[:, :, 0], pair(et)[:, :, 1], ALU.mult).then_inc(s_qc, 1)
                dve.wait_ge(s_eq, 2 * g + 1)
                dve.wait_ge(s_jact, emptied(at["q", g])[1])
                dve.tensor_tensor(qm[:, c], qT[:, c], eq[:, :], ALU.mult).then_inc(s_qm, 1)
                dve.wait_ge(s_qm, g + 1)
                dve.wait_ge(s_scq, 4 * (g + 1))
                dve.tensor_tensor(sub3(qc[:, c], SUB), sub3(qm[:, c], SUB), wide(scq[:, n], SUB), ALU.mult).then_inc(s_qc, 1)
                dve.tensor_tensor(qx[:, g * TG:(g + 1) * TG, :], sub3(qm[:, c], SUB)[:, 1::2, :],
                                  wide(em[:, n][:, 1::2], SUB), ALU.mult).then_inc(s_qc, 1)
                if g == 0:
                    dve.wait_ge(s_wo, 16 * (1 + P // dv))
                    dve.tensor_scalar(wo_sb[:, :, :], wo_in[:, :, :], gnorm_sb[:, 0:1], None, ALU.mult).then_inc(s_wo2, 1)
            dve.wait_ge(s_span0, 2 * NG)
            dve.tensor_reduce(widest[:, :], span[:, :, :].rearrange("p a n -> p (a n)"), AX_X, ALU.max).then_inc(s_widest, 1)
            dve.wait_ge(s_job, at["b1T", 0] + 1)
            dve.tensor_copy(b1_sb[:, :, :].rearrange("p e j -> p (e j)"), bank_of("b1T", 0)[:, 0:E * HC]).then_inc(s_jdve, 1)
            dve.wait_ge(s_job, at["span", 0] + 1)
            dve.tensor_reduce(worst[:, :], bank_of("span", 0)[0:1, 0:P], AX_X, ALU.max).then_inc(s_jdve, 1)
            dve.wait_ge(s_jdve, emptied(at["span", 0])[1])
            dve.tensor_scalar(wide_flag[:, :], worst[:, :], SAFE * GATE_NORMALIZER, None, ALU.is_gt).then_inc(s_flag, 1)
            for g in range(2 * NG):
                dve.wait_ge(s_job, at["v", g] + 1)
                dve.tensor_copy(v_sb[:, 2 * g:2 * g + 2, :], bank_of("v", g)[:, :].rearrange("p (t v) -> p t v", v=DV)).then_inc(s_jdve, 1)

            def mask_scores(t):
                dve.wait_ge(s_a, t + 1)
                dve.wait_ge(s_const, 2)
                if t >= 2:
                    dve.wait_ge(s_o, t - 1)
                for lo, hi, c0 in ((0, SUB, 0), (SUB, P, SUB)):
                    for h in range(HEADS):
                        dve.tensor_tensor(aT[lo:hi, t % 2, h, c0:P], bank[h][lo:hi, c0:P], causal[lo:hi, c0:P],
                                          ALU.mult).then_inc(s_aT, 1)

            def update_state(t):
                dve.wait_ge(s_kv, t + 1)
                if t >= 2:
                    dve.wait_ge(s_bd, t - 1)
                if t == 0:
                    dve.tensor_copy(state[:, 0, :], bank[7][:, 0:dv]).then_inc(s_state, 1)
                else:
                    dve.wait_ge(s_state, t)
                    dve.scalar_tensor_tensor(state[:, t % 2, :], state[:, (t - 1) % 2, :], tile_decay[:, t:t + 1],
                                             bank[7][:, 0:dv], ALU.mult, ALU.add).then_inc(s_state, 1)

            def norm_gate(t):
                dve.wait_ge(s_sq, t + 1)
                dve.tensor_reduce(ms[:, t % 2, :], sq[:, :].rearrange("p (h v) -> p h v", v=dv), AX_X, ALU.add).then_inc(s_ms0, 1)
                dve.wait_ge(s_ms0, t + 1)
                dve.tensor_scalar(ms[:, t % 2, :], ms[:, t % 2, :], 1.0 / dv, EPS, ALU.mult, ALU.add).then_inc(s_ms, 1)
                dve.wait_ge(s_rms, t + 1)
                dve.reciprocal(rrms[:, t % 2, :], rms[:, t % 2, :]).then_inc(s_rr, 1)
                dve.wait_ge(s_rr, t + 1)
                if t >= 2:
                    dve.wait_ge(s_ot, t - 1)
                for h in range(HEADS):
                    v = slice(h * dv, (h + 1) * dv)
                    dve.scalar_tensor_tensor(og[:, t % 2, v], bank[4 + t % 2][:, v], rrms[:, t % 2, h:h + 1],
                                             gate[:, t, v], ALU.mult, ALU.mult).then_inc(s_og, 1)

            def layer_norm1(t):
                b = t % 2
                dve.wait_ge(s_y, t + 1)
                dve.tensor_tensor(res[:, b, :], bank[4 + (t + 1) % 2][:, 0:D], x_sb[:, t, :], ALU.add).then_inc(s_res, 1)
                dve.wait_ge(s_res, t + 1)
                dve.bn_stats(stats[:, b, :], res[:, b, :]).then_inc(s_st, 1)
                dve.wait_ge(s_st, t + 1)
                dve.bn_aggr(mv[:, b, :], stats[:, b, :]).then_inc(s_mv, 1)
                dve.wait_ge(s_mv, t + 1)
                dve.tensor_scalar(mv[:, b, 1:2], mv[:, b, 1:2], EPS, None, ALU.add).then_inc(s_veps, 1)

            def layer_norm1_end(t):
                b = t % 2
                dve.wait_ge(s_std, t + 1)
                dve.reciprocal(rstd[:, b, :], std[:, b, :]).then_inc(s_rstd, 1)
                dve.wait_ge(s_rstd, t + 1)
                dve.tensor_scalar(x1[:, t, :], res[:, b, :], mv[:, b, 0:1], rstd[:, b, :], ALU.subtract, ALU.mult).then_inc(s_x1, 1)

            def take_x1T(t):
                dve.wait_ge(s_xt, t + 1)
                dve.tensor_copy(x1T[:, t * P:(t + 1) * P], bank[7][:, 0:P]).then_inc(s_x1T, 1)

            def take_scores(t):
                dve.wait_ge(s_sc, t + 1)
                if t == 0:
                    dve.wait_ge(s_router, 48)
                dve.tensor_tensor(score[:, t, :], bank[7][:, 0:E], br_sb[:, :], ALU.add).then_inc(s_route_in, 1)

            for i in range(T + 7):
                if i < T:
                    mask_scores(i)
                if 0 <= i - 1 < T:
                    update_state(i - 1)
                    norm_gate(i - 1)
                if 0 <= i - 3 < T:
                    layer_norm1(i - 3)
                    layer_norm1_end(i - 3)
                if 0 <= i - 4 < T:
                    take_x1T(i - 4)
                if 0 <= i - 5 < T:
                    take_scores(i - 5)

            dve.wait_ge(s_flag, 1)
            too_wide = dve.value_load(wide_flag[0:1, 0:1], min_val=0, max_val=1)
            with dve.If(too_wide):
                with dve.Fori(0, dv) as v:
                    turn = v * V_STEPS + V_BASE
                    dve.wait_ge(s_turn, turn)
                    dve.tensor_scalar(v_col, v_heads[:, :, :, bass.ds(v, 1)].to_broadcast([P, T, HEADS, dk]), 1.0, None, ALU.mult).then_inc(s_turn, 1)
                    for g in range(NG):
                        c = slice(g * GROUP, (g + 1) * GROUP)
                        dve.wait_ge(s_turn, turn + 2 + g)
                        dve.tensor_tensor(outer[:, c], kT[:, c], bank[g][:, :], ALU.mult).then_inc(s_turn, 1)
                    dve.wait_ge(s_turn, turn + 2 + NG)
                    dve.tensor_tensor_scan(states[:, :], decay[:, :], outer[:, :], 0.0, ALU.mult, ALU.add).then_inc(s_turn, 1)
                    for g in range(NG):
                        c = slice(g * GROUP, (g + 1) * GROUP)
                        dve.wait_ge(s_turn, turn + 3 + NG + g)
                        dve.tensor_tensor(q_states[:, c], qT[:, c], states[:, c], ALU.mult).then_inc(s_turn, 1)
                    dve.wait_ge(s_turn, turn + 4 + 2 * NG)
                    dve.tensor_scalar(v_heads[:, :, :, bass.ds(v, 1)].rearrange("p t h a -> p t (h a)"),
                                      bank[4][:, 0:T * HEADS].rearrange("p (t h) -> p t h", h=HEADS), 1.0, None, ALU.mult).then_inc(s_turn, 1)
                with dve.Fori(0, T) as t:
                    turn = t * T_STEPS + T_BASE

                    def one(a):
                        return a[:, bass.ds(t, 1), :].rearrange("p a v -> p (a v)")

                    dve.wait_ge(s_turn, turn + 1)
                    dve.tensor_reduce(ms[:, 0, :], sq[:, :].rearrange("p (h v) -> p h v", v=dv), AX_X, ALU.add).then_inc(s_turn, 1)
                    dve.wait_ge(s_turn, turn + 2)
                    dve.tensor_scalar(ms[:, 0, :], ms[:, 0, :], 1.0 / dv, EPS, ALU.mult, ALU.add).then_inc(s_turn, 1)
                    dve.wait_ge(s_turn, turn + 4)
                    dve.reciprocal(rrms[:, 0, :], rms[:, 0, :]).then_inc(s_turn, 1)
                    for h in range(HEADS):
                        c = slice(h * dv, (h + 1) * dv)
                        dve.wait_ge(s_turn, turn + 5 + h)
                        dve.scalar_tensor_tensor(og[:, 0, c], one(v_sb)[:, c], rrms[:, 0, h:h + 1], one(gate)[:, c],
                                                 ALU.mult, ALU.mult).then_inc(s_turn, 1)
                    dve.wait_ge(s_turn, turn + 12)
                    dve.tensor_tensor(res[:, 0, :], bank[5][:, 0:D], one(x_sb), ALU.add).then_inc(s_turn, 1)
                    dve.wait_ge(s_turn, turn + 13)
                    dve.bn_stats(stats[:, 0, :], res[:, 0, :]).then_inc(s_turn, 1)
                    dve.wait_ge(s_turn, turn + 14)
                    dve.sem_inc(s_pause, 1)
                    dve.bn_aggr(mv[:, 0, :], stats[:, 0, :]).then_inc(s_turn, 1)
                    dve.wait_ge(s_turn, turn + 15)
                    dve.tensor_scalar(mv[:, 0, 1:2], mv[:, 0, 1:2], EPS, None, ALU.add).then_inc(s_turn, 1)
                    dve.wait_ge(s_turn, turn + 17)
                    dve.reciprocal(rstd[:, 0, :], std[:, 0, :]).then_inc(s_turn, 1)
                    dve.wait_ge(s_turn, turn + 18)
                    dve.tensor_scalar(res[:, 1, :], res[:, 0, :], mv[:, 0, 0:1], rstd[:, 0, :], ALU.subtract, ALU.mult).then_inc(s_turn, 1)
                    dve.wait_ge(s_turn, turn + 20)
                    dve.tensor_scalar(one(x1), res[:, 1, :], 1.0, None, ALU.mult).then_inc(s_turn, 1)
                    dve.wait_ge(s_turn, turn + 21)
                    dve.tensor_scalar(x1T[:, bass.ds(t * P, P)], bank[7][:, 0:P], 1.0, None, ALU.mult).then_inc(s_turn, 1)
                    dve.wait_ge(s_turn, turn + 22)
                    dve.tensor_copy(kcT[:, 0, :], bank[7][:, 0:P]).then_inc(s_turn, 1)
                    dve.wait_ge(s_turn, turn + 24)
                    dve.tensor_tensor(one(score), bank[7][:, 0:E], br_sb[:, :], ALU.add).then_inc(s_turn, 1)
                dve.wait_ge(s_turn, T_BASE + T * T_STEPS)

            step = [0]

            def chain(ins):
                step[0] += 1
                ins.then_inc(s_route, 1)
                dve.wait_ge(s_route, step[0])

            dve.wait_ge(s_route_in, T)
            dve.wait_ge(s_const, 7)
            rank = rank_e[:, :].unsqueeze(1).to_broadcast([P, T, E])

            def pick(scores, top, one_hot):
                chain(dve.tensor_reduce(top[:, :], scores[:, :, :], AX_X, ALU.max))
                chain(dve.tensor_tensor(hit[:, :, :], scores[:, :, :], wide(top[:, :], E), ALU.is_equal))
                chain(dve.tensor_tensor(pri[:, :, :], hit[:, :, :], rank, ALU.mult))
                chain(dve.tensor_reduce(best[:, :], pri[:, :, :], AX_X, ALU.max))
                chain(dve.tensor_tensor(one_hot[:, :, :], pri[:, :, :], wide(best[:, :], E), ALU.is_equal))

            pick(score, top1, first)
            chain(dve.scalar_tensor_tensor(score2[:, :, :], first[:, :, :], -BIG, score[:, :, :], ALU.mult, ALU.add))
            pick(score2, top2, second)
            chain(dve.tensor_tensor(gap[:, :], top2[:, :], top1[:, :], ALU.subtract))
            assert step[0] == 12
            dve.wait_ge(s_egap, 1)
            chain(dve.tensor_scalar(wsum[:, :], egap[:, :], 1.0, None, ALU.add))
            chain(dve.reciprocal(wt1[:, :], wsum[:, :]))
            chain(dve.tensor_tensor(wt2[:, :], egap[:, :], wt1[:, :], ALU.mult))
            chain(dve.tensor_tensor(first[:, :, :], first[:, :, :], wide(wt1[:, :], E), ALU.mult))
            chain(dve.tensor_tensor(second[:, :, :], second[:, :, :], wide(wt2[:, :], E), ALU.mult))
            dve.tensor_tensor(weight[:, :, :], first[:, :, :], second[:, :, :], ALU.add).then_inc(s_weight, 1)
            for g in range(NG):
                dve.wait_ge(s_wt, g + 1)
                dve.tensor_copy(weightT[:, g * GROUP:(g + 1) * GROUP], bank[6][0:E, :]).then_inc(s_wT, 1)
                dve.wait_ge(s_bias, g + 1)
                dve.tensor_tensor(acc[:, g * TG:(g + 1) * TG, :], bank[7][:, :].rearrange("p (t d) -> p t d", d=D),
                                  x1[:, g * TG:(g + 1) * TG, :], ALU.add).then_inc(s_acc0, 1)

            def hidden(k):
                e, g = FFN[k]
                for j in range(1, HC, 2):
                    dve.wait_ge(s_h, k * HC + j + 1)
                    if k >= 2:
                        dve.wait_ge(s_ye, (k - 1) * TG)
                    dve.tensor_scalar(hT[:, k % 2, j, :], bank[j][:, :], b1_sb[:, e, j:j + 1], 0.0, ALU.add, ALU.max).then_inc(s_hd, 1)

            def accumulate(k):
                e, g = FFN[k]
                for u in range(TG):
                    t = g * TG + u
                    dve.wait_ge(s_ye, k * TG + u + 1)
                    if u == 0:
                        if e:
                            dve.wait_ge(s_acc, (k - NG + 1) * TG)
                        else:
                            dve.wait_ge(s_acc0, NG)
                    dve.scalar_tensor_tensor(acc[:, t, :], bank[4 + (k * TG + u) % 4][:, 0:D], weight[:, t, e:e + 1],
                                             acc[:, t, :], ALU.mult, ALU.add).then_inc(s_acc, 1)

            hidden(0)
            for k in range(len(FFN)):
                if k + 1 < len(FFN):
                    hidden(k + 1)
                accumulate(k)
                if FFN[k][0] == E - 1:
                    for u in range(TG):
                        t = FFN[k][1] * TG + u
                        dve.wait_ge(s_acc, k * TG + u + 1)
                        dve.bn_stats(fstats[:, t, :], acc[:, t, :]).then_inc(s_fst, 1)
                        dve.wait_ge(s_fst, t + 1)
                        dve.bn_aggr(fmv[:, t, :], fstats[:, t, :]).then_inc(s_fmv, 1)
                        dve.wait_ge(s_fmv, t + 1)
                        dve.tensor_scalar(fmv[:, t, 1:2], fmv[:, t, 1:2], EPS, None, ALU.add).then_inc(s_fve, 1)
            for t in range(T):
                dve.wait_ge(s_fstd, t + 1)
                dve.reciprocal(frstd[:, t, :], fstd[:, t, :]).then_inc(s_frs, 1)
                dve.wait_ge(s_frs, t + 1)
                dve.tensor_scalar(result[:, t, :], acc[:, t, :], fmv[:, t, 0:1], frstd[:, t, :], ALU.subtract, ALU.mult).then_inc(s_res2, 1)

        @block.tensor
        def _(pe):
            mm = nc.tensor.matmul

            def job(kind, g):
                i = at[kind, g]
                if i >= 8:
                    pe.wait_ge(*emptied(i - 8))
                b = bank[i % 8]
                c = slice(g * GROUP, (g + 1) * GROUP)
                if kind == "xT":
                    pe.wait_ge(s_x[g], 16)
                    if g == 0:
                        pe.wait_ge(s_const, 1)
                    for u in range(TG):
                        last = nc.tensor.transpose(b[:, u * P:(u + 1) * P], x_sb[:, g * TG + u, :], ident[:, :])
                elif kind == "wgk1T":
                    pe.wait_ge(s_gatew, 48)
                    last = nc.tensor.transpose(b[0:R, 0:P], wgk1_sb[:, :], ident[:, :])
                elif kind == "b1T":
                    pe.wait_ge(s_b1, 16)
                    last = nc.tensor.transpose(b[:, 0:E * HC], b1_in[:, :], ident[0:E * HC, 0:E * HC])
                elif kind == "span":
                    pe.wait_ge(s_widest, 1)
                    last = nc.tensor.transpose(b[0:1, 0:P], widest[:, :], ident[:, :])
                elif kind == "wgk":
                    pe.wait_ge(*emptied(at["wgk1T", 0]))
                    last = mm(b[:, 0:P], wgk1T[:, :], wgk2_sb[:, :], start=True, stop=True)
                elif kind == "z":
                    pe.wait_ge(*emptied(at["xT", g]))
                    pe.wait_ge(*emptied(at["wgk", 0]))
                    last = mm(b[:, :], wgk[:, :], xT[:, c], start=True, stop=True)
                elif kind in ("q", "k"):
                    if g == 0:
                        pe.wait_ge(s_projw, 32)
                    last = mm(b[:, :], (wq_sb if kind == "q" else wk_sb)[:, :], xT[:, c], start=True, stop=True)
                else:
                    if g == 0:
                        pe.wait_ge(s_vgw, 32)
                    w = wv_sb if kind == "v" else wg_sb
                    for u in range(2):
                        t = 2 * g + u
                        last = mm(b[:, u * DV:(u + 1) * DV], xT[:, t * P:(t + 1) * P], w[:, :], start=True, stop=True)
                last.then_inc(s_job, 1)

            for kind, g, _ in jobs:
                job(kind, g)
            pe.wait_ge(s_jact, n_act)
            pe.wait_ge(s_jdve, n_dve)

            def scores(t):
                g = t // TG
                c = t * P
                if t % TG == 0:
                    pe.wait_ge(s_qm, g + 1)
                    pe.wait_ge(s_km, g + 1)
                    pe.wait_ge(s_qc, 3 * (g + 1))
                    pe.wait_ge(s_kc, 2 * (g + 1))
                if t:
                    pe.wait_ge(s_aT, 8 * t)
                for h in range(HEADS):
                    r = slice(h * dk, (h + 1) * dk)
                    mm(bank[h][0:SUB, 0:SUB], km[r, c:c + SUB], qm[r, c:c + SUB], start=True, stop=True)
                for h in range(HEADS):
                    r = slice(h * dk, (h + 1) * dk)
                    mm(bank[h][0:SUB, SUB:P], kx[r, t, :], qx[r, t, :], start=True, stop=True)
                for h in range(HEADS):
                    r = slice(h * dk, (h + 1) * dk)
                    last = mm(bank[h][SUB:P, SUB:P], km[r, c + SUB:c + P], qm[r, c + SUB:c + P], start=True, stop=True)
                last.then_inc(s_a, 1)
                if t:
                    pe.wait_ge(s_kcT, t)
                if t >= 3:
                    pe.wait_ge(s_oT, t - 2)
                nc.tensor.transpose(bank[6][:, 0:P], kc[:, c:c + P], ident[:, :]).then_inc(s_kt, 1)

            def update(t):
                pe.wait_ge(s_kcT, t + 1)
                if t:
                    pe.wait_ge(s_state, t)
                if t >= 4:
                    pe.wait_ge(s_x1T, t - 3)
                if t >= 5:
                    pe.wait_ge(s_route_in, t - 4)
                for h in range(HEADS):
                    last = mm(bank[7][h * dk:(h + 1) * dk, 0:dv], kcT[:, t % 2, h * dk:(h + 1) * dk],
                              v_sb[:, t, h * dv:(h + 1) * dv], start=True, stop=True)
                last.then_inc(s_kv, 1)

            def attend(t):
                b = bank[4 + t % 2]
                if t >= 2:
                    pe.wait_ge(s_og, HEADS * (t - 1))
                if t >= 3:
                    pe.wait_ge(s_res, t - 2)
                if t:
                    pe.wait_ge(s_bd, t)
                    mm(b[:, 0:DV], qc[:, t * P:(t + 1) * P], state_bd[:, t % 2, :, :].rearrange("p h v -> p (h v)"),
                       start=True, stop=True, skip_group_check=True)
                pe.wait_ge(s_aT, 8 * (t + 1))
                for h in range(HEADS):
                    last = mm(b[:, h * dv:(h + 1) * dv], aT[:, t % 2, h, :], v_sb[:, t, h * dv:(h + 1) * dv],
                              start=(t == 0 and h == 0), stop=True, skip_group_check=True)
                last.then_inc(s_o, 1)

            def transpose_o(t):
                pe.wait_ge(s_og, HEADS * (t + 1))
                pe.wait_ge(s_kcT, min(t + 3, T))
                if t:
                    pe.wait_ge(s_oT, t)
                for c in range(DVC):
                    last = nc.tensor.transpose(bank[6][:, c * P:(c + 1) * P], og[:, t % 2, c * P:(c + 1) * P], ident[:, :])
                last.then_inc(s_ot, 1)

            def project_out(t):
                if t == 0:
                    pe.wait_ge(s_wo2, 1)
                pe.wait_ge(s_oT, t + 1)
                pe.wait_ge(s_og, HEADS * min(t + 2, T))
                for c in range(DVC):
                    last = mm(bank[4 + (t + 1) % 2][:, 0:D], oT[:, t % 2, c, :], wo_sb[:, c, :],
                              start=(c == 0), stop=(c == DVC - 1))
                last.then_inc(s_y, 1)

            def transpose_x1(t):
                pe.wait_ge(s_x1, t + 1)
                pe.wait_ge(s_state, min(t + 4, T))
                if t >= 1:
                    pe.wait_ge(s_x1T, t)
                if t >= 2:
                    pe.wait_ge(s_route_in, t - 1)
                nc.tensor.transpose(bank[7][:, 0:P], x1[:, t, :], ident[:, :]).then_inc(s_xt, 1)

            def route(t):
                if t == 0:
                    pe.wait_ge(s_router, 48)
                pe.wait_ge(s_x1T, min(t + 2, T))
                if t:
                    pe.wait_ge(s_route_in, t)
                mm(bank[7][:, 0:E], x1T[:, t * P:(t + 1) * P], wr_sb[:, :], start=True, stop=True).then_inc(s_sc, 1)

            for i in range(T + 5):
                if i < T:
                    scores(i)
                if 0 <= i - 1 < T:
                    update(i - 1)
                    attend(i - 1)
                if 0 <= i - 2 < T:
                    transpose_o(i - 2)
                if 0 <= i - 3 < T:
                    project_out(i - 3)
                if 0 <= i - 4 < T:
                    transpose_x1(i - 4)
                if 0 <= i - 5 < T:
                    route(i - 5)

            def hidden(k):
                e, g = FFN[k]
                if k == 0:
                    pe.wait_ge(s_ffn1, 16)
                for j in range(HC):
                    if k:
                        if j % 2 == 0:
                            pe.wait_ge(s_ha, (k - 1) * HC // 2 + j // 2 + 1)
                        else:
                            pe.wait_ge(s_hd, (k - 1) * HC // 2 + j // 2 + 1)
                    mm(bank[j][:, :], w1_sb[:, e, j * P:(j + 1) * P], x1T[:, g * GROUP:(g + 1) * GROUP],
                       start=True, stop=True).then_inc(s_h, 1)

            def expert_out(k):
                e, g = FFN[k]
                if k == 0:
                    pe.wait_ge(s_ffn2, 16)
                pe.wait_ge(s_ha, (k + 1) * HC // 2)
                pe.wait_ge(s_hd, (k + 1) * HC // 2)
                for u in range(TG):
                    n = k * TG + u
                    if n >= 4:
                        pe.wait_ge(s_acc, n - 3)
                    for j in range(HC):
                        last = mm(bank[4 + n % 4][:, 0:D], hT[:, k % 2, j, u * P:(u + 1) * P], w2_sb[:, e, j, :],
                                  start=(j == 0), stop=(j == HC - 1))
                    last.then_inc(s_ye, 1)

            pe.wait_ge(s_flag, 1)
            too_wide = pe.value_load(wide_flag[0:1, 0:1], min_val=0, max_val=1)
            with pe.If(too_wide):
                with pe.Fori(0, dv) as v:
                    turn = v * V_STEPS + V_BASE
                    pe.wait_ge(s_turn, turn + 1)
                    for t in range(T):
                        last = mm(bank[t // TG][:, (t % TG) * P:(t % TG + 1) * P],
                                  v_col[:, t, :, :].rearrange("p h k -> p (h k)"),
                                  ident[:, :], start=True, stop=True)
                    last.then_inc(s_turn, 1)
                    pe.wait_ge(s_turn, turn + 3 + 2 * NG)
                    for t in range(T):
                        last = mm(bank[4][:, t * HEADS:(t + 1) * HEADS], q_states[:, t * P:(t + 1) * P], head_pick,
                                  start=True, stop=True)
                    last.then_inc(s_turn, 1)
                with pe.Fori(0, T) as t:
                    turn = t * T_STEPS + T_BASE
                    pe.wait_ge(s_turn, turn + 9)
                    for c in range(DVC):
                        last = nc.tensor.transpose(bank[6][:, c * P:(c + 1) * P], og[:, 0, c * P:(c + 1) * P], ident[:, :])
                    last.then_inc(s_turn, 1)
                    pe.wait_ge(s_turn, turn + 11)
                    for c in range(DVC):
                        last = mm(bank[5][:, 0:D], oT[:, 0, c, :], wo_sb[:, c, :], start=(c == 0), stop=(c == DVC - 1))
                    last.then_inc(s_turn, 1)
                    pe.wait_ge(s_turn, turn + 19)
                    nc.tensor.transpose(bank[7][:, 0:P], res[:, 1, :], ident[:, :]).then_inc(s_turn, 1)
                    pe.wait_ge(s_turn, turn + 23)
                    mm(bank[7][:, 0:E], kcT[:, 0, :], wr_sb[:, :], start=True, stop=True).then_inc(s_turn, 1)
            hidden(0)
            pe.wait_ge(s_weight, 1)
            for g in range(NG):
                if g:
                    pe.wait_ge(s_wT, g)
                for u in range(TG):
                    last = nc.tensor.transpose(bank[6][0:E, u * P:(u + 1) * P], weight[:, g * TG + u, :], ident[:, :])
                last.then_inc(s_wt, 1)
                pe.wait_ge(s_wT, g + 1)
                if g:
                    pe.wait_ge(s_acc0, g)
                for u in range(TG):
                    last = mm(bank[7][:, u * D:(u + 1) * D], weightT[:, (g * TG + u) * P:(g * TG + u + 1) * P], b2_sb[:, :],
                              start=True, stop=True)
                last.then_inc(s_bias, 1)
            pe.wait_ge(s_acc0, NG)
            for k in range(len(FFN)):
                if k + 1 < len(FFN):
                    hidden(k + 1)
                expert_out(k)

_INS = ['L0_attn_x', 'L0_attn_Wq', 'L0_attn_Wk', 'L0_attn_Wv', 'L0_attn_Wg', 'L0_attn_Wgk1', 'L0_attn_Wgk2', 'L0_attn_bgk2', 'L0_attn_Wo', 'L0_attn_g_norm_weight', 'L0_ffn_Wr', 'L0_ffn_br', 'L0_ffn_W1', 'L0_ffn_b1', 'L0_ffn_W2', 'L0_ffn_b2']
_OUTS = [((1, 2048, 128), 'float32')]


def kernel(**inputs):
    import numpy as _np
    import concourse.bacc as _bacc
    from concourse import mybir as _mybir
    from concourse.bass_utils import run_bass_kernel_spmd as _run

    nc = _bacc.Bacc("TRN2", target_bir_lowering=False, num_devices=1)
    arrays, args = {}, []
    for name in _INS:
        a = _np.ascontiguousarray(inputs[name])
        arrays[f"in_{name}_dram"] = a
        args.append(nc.dram_tensor(f"in_{name}_dram", a.shape, _mybir.dt.from_np(a.dtype), kind="ExternalInput").ap())
    for i, (shape, dtype) in enumerate(_OUTS):
        dt = _mybir.dt.from_np(_np.dtype(dtype))
        args.append(nc.dram_tensor(f"out_{i}_dram", shape, dt, kind="ExternalOutput").ap())
    build(nc, *args)
    r = _run(nc, [arrays], core_ids=[0])
    got = tuple(r.results[0][f"out_{i}_dram"] for i in range(len(_OUTS)))
    return got[0]
```

```python
from contextlib import ExitStack

import concourse.bass as bass
from concourse import mybir

F32 = mybir.dt.float32
I32 = mybir.dt.int32
U32 = mybir.dt.uint32
ACT = mybir.ActivationFunctionType
ALU = mybir.AluOpType
AX_X = mybir.AxisListType.X

P = 128
HEADS = 4
EPS = 1e-5
GATE_NORMALIZER = 16.0
GROUP = 512
SAFE = 80.0
TOP = 2
AHEAD = 6


def build(nc, x, Wq, Wk, Wv, Wg, Wgk1, Wgk2, bgk2, Wo, g_norm, Wr, br, W1, b1, W2, b2, out):
    _, N, D = x.shape
    R = Wgk1.shape[1]
    DV = Wv.shape[1]
    E = Wr.shape[1]
    H = W1.shape[2]
    dk = P // HEADS
    dv = DV // HEADS
    T = N // P
    NG = N // GROUP
    TG = GROUP // P
    MID = P // 2 - 1
    HC = H // P
    DVC = DV // P
    NB = T // 2
    CAP = N + P
    ROW = D + 2
    SLOTS = (TOP * N - E) // P + E
    assert D == P and Wq.shape[1] == P and T % 2 == 0 and SLOTS % 3 == 0 and SLOTS >= 9

    x_tok = x.rearrange("a (t p) d -> p (a t) d", p=P)
    out_tok = out.rearrange("a (t p) d -> p (a t) d", p=P)
    rows = nc.dram_tensor("expert_rows", [E * CAP, ROW], F32, kind="Internal").ap()
    results = nc.dram_tensor("expert_results", [TOP * N, D], F32, kind="Internal").ap()

    with ExitStack() as ctx:
        def sb(name, shape, dt=F32):
            return ctx.enter_context(nc.sbuf_tensor(name, shape, dt))

        def sem(name):
            return ctx.enter_context(nc.semaphore(name))

        x_sb = sb("x_sb", [P, T, D])
        wq_sb = sb("wq_sb", [P, P])
        wk_sb = sb("wk_sb", [P, P])
        wv_sb = sb("wv_sb", [P, DV])
        wg_sb = sb("wg_sb", [P, DV])
        wgk1_sb = sb("wgk1_sb", [P, R])
        wgk2_sb = sb("wgk2_sb", [R, P])
        bgk2_sb = sb("bgk2_sb", [P, 1])
        wo_in = sb("wo_in", [P, DVC, D])
        gnorm_sb = sb("gnorm_sb", [P, 1])
        wr_sb = sb("wr_sb", [P, E])
        br_sb = sb("br_sb", [P, E])
        b1_in = sb("b1_in", [E * HC, P])
        b1_sb = sb("b1_sb", [P, E * HC])
        w2_sb = sb("w2_sb", [P, E, HC * D])
        b2_sb = sb("b2_sb", [P, E, D])
        ident = sb("ident", [P, P])
        causal = sb("causal", [P, P])
        keep = sb("keep", [P, P], I32)
        before = sb("before", [P, P])
        ones = sb("ones", [P, P])
        head_pick = sb("head_pick", [P, HEADS])
        block_ones = sb("block_ones", [P, P])
        seg = sb("seg", [P, GROUP])
        eps_sb = sb("eps_sb", [P, 1])
        expert_id = sb("expert_id", [P, E])
        expert_row = sb("expert_row", [P, E])
        full_tiles = sb("full_tiles", [1, E, T])
        slot_id = sb("slot_id", [1, SLOTS])
        pad_row = sb("pad_row", [P, ROW])
        xT = sb("xT", [P, N])
        wgk1T = sb("wgk1T", [R, P])
        wgk = sb("wgk", [P, P])
        wo_sb = sb("wo_sb", [P, DVC, D])
        qT = sb("qT", [P, N])
        kT = sb("kT", [P, N])
        gT = sb("gT", [P, N])
        cum = sb("cum", [P, N])
        dist = sb("dist", [P, 2, GROUP])
        eq = sb("eq", [P, 2, GROUP])
        ek = sb("ek", [P, 2, GROUP])
        rest = sb("rest", [P, T])
        em = sb("em", [P, T])
        er = sb("er", [P, T])
        tile_decay = sb("tile_decay", [P, T])
        qm = sb("qm", [P, N])
        km = sb("km", [P, N])
        soft, zb = qm, km
        qc = sb("qc", [P, N])
        kc = sb("kc", [P, N])
        v_sb = sb("v_sb", [P, T, DV])
        gate = sb("gate", [P, DVC, N])
        aT = sb("aT", [P, 2, HEADS, P])
        kcT = sb("kcT", [P, 2, P])
        state = sb("state", [P, 2, DV])
        sq = sb("sq", [P, 2, DVC, P])
        lrms = sb("lrms", [P, DVC, P])
        rrms = sb("rrms", [P, 2, DVC, P])
        rgate = sb("rgate", [P, 2, DVC, P])
        ogT = sb("ogT", [P, 2, DVC, P])
        res = sb("res", [P, 2, D])
        stats = sb("stats", [P, 2, 6])
        mv = sb("mv", [P, 2, 2])
        lstd = sb("lstd", [P, 2, 1])
        rstd = sb("rstd", [P, 2, 1])
        x1T = sb("x1T", [P, 2, P])
        xr = sb("xr", [P, T, TOP, ROW])
        score = sb("score", [P, T, E])
        top8 = sb("top8", [P, T, 8])
        top_at = sb("top_at", [P, T, 8], U32)
        top_f = sb("top_f", [P, T, TOP])
        hot = sb("hot", [P, T, TOP, E])
        hit = sb("hit", [P, T, E])
        so_far = sb("so_far", [P, T + 1, E])
        gap = sb("gap", [P, T])
        egap = sb("egap", [P, T])
        wsum = sb("wsum", [P, T])
        place = sb("place", [P, T, E])
        placed = sb("placed", [P, T, TOP, E])
        slot_f = sb("slot_f", [P, T, TOP])
        slot = sb("slot", [P, T, TOP], U32)
        count = sb("count", [1, E])
        more = sb("more", [1, E, T])
        ntile = sb("ntile", [1, E])
        ends = sb("ends", [1, E])
        past = sb("past", [1, SLOTS, E])
        past_tiles = sb("past_tiles", [1, SLOTS, E])
        slot_e = sb("slot_e", [1, SLOTS])
        slot_t = sb("slot_t", [1, SLOTS])
        slot_row = sb("slot_row", [1, SLOTS])
        used = sb("used", [1, SLOTS])
        slot_table = sb("slot_table", [1, 2, SLOTS])
        table = sb("table", [1, 2, SLOTS], I32)
        xg = sb("xg", [P, AHEAD, ROW])
        w1_buf = [m[:, n * H:(n + 1) * H] for m in (km, qm) for n in range(AHEAD // 2)]
        xgT, yb, yw = (kT[:, 3 * D * n:3 * D * (n + 1)].rearrange("p (u d) -> p u d", d=D) for n in range(3))
        hT = gT[:, 0:3 * H].rearrange("p (u j t) -> p u j t", j=HC, t=P)
        dest = sb("dest", [P, 3], U32)
        ysum = gate[:, :, :].rearrange("p c n -> p (c n)").rearrange("p (t d) -> p t d", d=TOP * D)
        assert DV == TOP * D
        acc = xT[:, :].rearrange("p (t d) -> p t d", d=D)
        fstats = sb("fstats", [P, T, 6])
        fmv = sb("fmv", [P, T, 2])
        flog = sb("flog", [P, T])
        frstd = sb("frstd", [P, T])
        fshift = sb("fshift", [P, T])
        result = x_sb
        span = sb("span", [P, 2, T])
        widest = sb("widest", [P, 1])
        worst = sb("worst", [1, 1])
        wide_flag = sb("wide_flag", [1, 1], I32)
        decay, outer, states, q_states = qm, km, kc, kc
        v_col = xr[:, :, 0, 0:D].rearrange("p t (h k) -> p t h k", k=dk)
        v_heads = v_sb[:, :, :].rearrange("p t (h v) -> p t h v", v=dv)

        psum = ctx.enter_context(nc.psum_tensor("psum", [P, 8, 512], F32))
        bank = [psum[:, i, :] for i in range(8)]

        s_x = [sem(f"x_loaded{g}") for g in range(NG)]
        s_gatew = sem("gate_weights_loaded")
        s_projw = sem("projection_weights_loaded")
        s_vgw = sem("value_weights_loaded")
        s_wo = sem("wo_loaded")
        s_router = sem("router_loaded")
        s_b1 = sem("b1_loaded")
        s_w2 = sem("w2_loaded")
        s_seed = sem("constants_zeroed")
        s_const = sem("constants_made")
        s_dinit = sem("vector_buffers_set")
        s_job = sem("projection_in_psum")
        s_jact = sem("act_emptied_bank")
        s_jdve = sem("dve_emptied_bank")
        s_wo2 = sem("wo_scaled")
        s_abs = sem("abs_done")
        s_exp = sem("exp_done")
        s_soft = sem("softplus_done")
        s_g = sem("gate_log_done")
        s_cum = sem("cumsum_done")
        s_rest = sem("rest_done")
        s_span = sem("decay_spans_done")
        s_dist0 = sem("distance_done")
        s_dist = sem("distance_clamped")
        s_small = sem("tile_factors_done")
        s_eq = sem("decay_factors_done")
        s_qm = sem("qm_done")
        s_qc = sem("qc_done")
        s_km = sem("km_done")
        s_kc = sem("kc_done")
        s_widest = sem("widest_span_of_channels")
        s_flag = sem("range_flag_ready")
        s_turn = sem("general_path_turn")
        s_a = sem("scores_in_psum")
        s_aT = sem("scores_masked")
        s_act_bank = sem("act_bank_written")
        s_dve_bank = sem("dve_bank_written")
        s_kcT = sem("kc_copied")
        s_state = sem("state_updated")
        s_o = sem("o_in_psum")
        s_sq = sem("o_squared")
        s_lrms = sem("log_rms_done")
        s_rr = sem("rrms_done")
        s_rg = sem("gate_over_rms_done")
        s_og = sem("o_gated")
        s_res = sem("residual_done")
        s_st = sem("stats_done")
        s_mv = sem("mean_var_done")
        s_lstd = sem("log_std_done")
        s_rstd = sem("rstd_done")
        s_x1 = sem("x1_done")
        s_x1T = sem("x1T_copied")
        s_score = sem("score_kept")
        s_top = sem("top8_found")
        s_topat = sem("top_indices_found")
        s_topf = sem("top_indices_as_float")
        s_hot = sem("one_hot_done")
        s_hit = sem("hits_done")
        s_sofar = sem("running_hits_done")
        s_gap = sem("gap_done")
        s_egap = sem("exp_gap_done")
        s_wsum = sem("weight_sum_done")
        s_w1st = sem("first_weight_done")
        s_weight = sem("weights_done")
        s_place0 = sem("places_taken")
        s_placed = sem("places_picked")
        s_slotf = sem("slots_as_float")
        s_slot = sem("slots_done")
        s_xcopy = sem("second_rows_copied")
        s_pad = sem("rows_padded")
        s_scat = sem("rows_scattered")
        s_tab = sem("table_step")
        s_table = sem("table_done")
        s_xg = [sem(f"rows_gathered{u}") for u in range(AHEAD)]
        s_w1 = [sem(f"w1_gathered{u}") for u in range(AHEAD)]
        s_gt = sem("rows_transposed")
        s_gT = sem("rows_transposed_copied")
        s_ha = sem("hidden_lower_in_psum")
        s_hb = sem("hidden_upper_in_psum")
        s_hTa = sem("hidden_lower_done")
        s_hTb = sem("hidden_upper_done")
        s_ye = sem("expert_out_in_psum")
        s_yb = sem("expert_out_biased")
        s_yw = sem("expert_out_weighted")
        s_dest = sem("destinations_done")
        s_out = [sem(f"results_scattered{u}") for u in range(3)]
        s_ysum = [sem(f"results_loaded{g}") for g in range(NG)]
        s_acc0 = sem("first_result_added")
        s_acc = sem("second_result_added")
        s_fst = sem("final_stats")
        s_fmv = sem("final_mean_var")
        s_flog = sem("final_log")
        s_frs = sem("final_rstd")
        s_fshift = sem("final_shift")
        s_result = sem("result_done")
        s_stored = sem("stored")

        jobs = [("xT", 0, "dve"), ("wgk1T", 0, "dve"), ("wgk", 0, "dve")]
        for g in range(1, NG):
            jobs += [("xT", g, "act" if g % 2 else "dve"), ("z", g - 1, "dve")]
        jobs += [("z", NG - 1, "dve")]
        for g in range(NG):
            jobs += [("q", g, "act"), ("k", g, "act"), ("v", 2 * g, "dve"), ("v", 2 * g + 1, "dve")]
        jobs += [("g", g, "act") for g in range(NG)]
        jobs += [("b1T", 0, "dve"), ("span", 0, "dve")]
        jobs += [("g", g, "act") for g in range(NG, 2 * NG)]
        at = {job[:2]: i for i, job in enumerate(jobs)}

        def emptied(i):
            engine = jobs[i][2]
            return (s_jact if engine == "act" else s_jdve), sum(j[2] == engine for j in jobs[:i + 1])

        def bank_of(kind, g):
            return bank[at[kind, g] % 8]

        n_act = sum(j[2] == "act" for j in jobs)
        n_dve = len(jobs) - n_act

        def tiles(ap):
            return ap.rearrange("p (n c) -> p n c", c=P)

        def wide(ap, n):
            return ap.unsqueeze(2).to_broadcast([ap.shape[0], ap.shape[1], n])

        V_STEPS = 5 + 2 * NG
        V_END = 1 + dv * V_STEPS

        AGE_O, AGE_GATE, AGE_OUT, AGE_X1T, AGE_ROUTE, AGE_PLACE = 1, 2, 3, 4, 5, 6
        ROUNDS = T + AGE_PLACE

        def factor_round(g):
            return (TG - 1) * (g - 1)

        groups_begun = {factor_round(g): g for g in range(1, NG)}
        groups_ended = {factor_round(g) + 1: g for g in range(1, NG)}

        def at_age(i, age):
            return i - age if 0 <= i - age < T else None

        def batch_at(i, lag):
            t = i - lag
            return t // 2 if 0 <= t < T and t % 2 else None

        block = ctx.enter_context(nc.Block())

        @block.sync
        def _(sp):
            for g in range(NG):
                sp.dma_start(x_sb[:, g * TG:(g + 1) * TG, :], x_tok[:, g * TG:(g + 1) * TG, :]).then_inc(s_x[g], 16)
            sp.dma_start(wv_sb[:, :], Wv).then_inc(s_vgw, 16)
            sp.dma_start(wg_sb[:, :], Wg).then_inc(s_vgw, 16)
            sp.dma_start(wo_in[:, :, :], Wo.rearrange("(c p) d -> p c d", p=P)).then_inc(s_wo, 16)
            for c in range(P // dv):
                sp.dma_start(gnorm_sb[c * dv:(c + 1) * dv, :], g_norm.rearrange("(p a) -> p a", a=1)).then_inc(s_wo, 16)
            sp.wait_ge(s_const, 4)
            for e in range(E):
                sp.dma_start(rows[e * CAP:(e + 1) * CAP, :].rearrange("(n p) c -> p n c", p=P),
                             pad_row[:, :].unsqueeze(1).to_broadcast([P, CAP // P, ROW])).then_inc(s_pad, 16)
            sp.dma_start(w2_sb[:, :, :].rearrange("p e (j d) -> p e j d", d=D),
                         W2.rearrange("e (j p) d -> p e j d", p=P)).then_inc(s_w2, 16)
            sp.dma_start(b2_sb[:, :, :], b2.partition_broadcast(P)).then_inc(s_w2, 16)

            sp.wait_ge(s_table, 1)
            for i in range(SLOTS):
                u = i % AHEAD
                e = sp.value_load(table[0:1, 0, i:i + 1], min_val=0, max_val=E - 1)
                r = sp.value_load(table[0:1, 1, i:i + 1], min_val=0, max_val=E * CAP - P)
                if i >= AHEAD:
                    sp.wait_ge(s_hb, i - AHEAD + 1)
                sp.dma_start(w1_buf[u], W1[bass.ds(e, 1), :, :].rearrange("a p h -> p (a h)")).then_inc(s_w1[u], 16)
                if i == 0:
                    sp.wait_ge(s_scat, 16 * T * TOP)
                if i >= AHEAD:
                    sp.wait_ge(s_yw, i - AHEAD + 1)
                    sp.wait_ge(s_dest, i - AHEAD + 1)
                sp.dma_start(xg[:, u, :], rows[bass.ds(r, P), :]).then_inc(s_xg[u], 16)
            for u in range(3):
                sp.wait_ge(s_out[u], 16 * (SLOTS // 3))
            for g in range(NG):
                sp.dma_start(ysum[:, g * TG:(g + 1) * TG, :],
                             results[g * GROUP * TOP:(g + 1) * GROUP * TOP, :].rearrange("(t p k) d -> p t (k d)", p=P, k=TOP)).then_inc(s_ysum[g], 16)
            for g in range(NG):
                sp.wait_ge(s_result, (g + 1) * TG)
                sp.dma_start(out_tok[:, g * TG:(g + 1) * TG, :], result[:, g * TG:(g + 1) * TG, :]).then_inc(s_stored, 16)
            sp.wait_ge(s_stored, 16 * NG)

        @block.gpsimd
        def _(pool):
            pool.memset(ident[:, :], 0.0).then_inc(s_seed, 1)
            pool.memset(causal[:, :], 1.0).then_inc(s_seed, 1)
            pool.memset(before[:, :], 1.0).then_inc(s_seed, 1)
            pool.memset(head_pick[:, :], 0.0).then_inc(s_seed, 1)
            pool.memset(block_ones[:, :], 0.0).then_inc(s_seed, 1)
            pool.memset(pad_row[:, :], 0.0).then_inc(s_seed, 1)
            n = [0]

            def const(ins):
                n[0] += 1
                ins.then_inc(s_const, 1)
                pool.wait_ge(s_const, n[0])

            pool.wait_ge(s_seed, 6)
            const(pool.affine_select(out=ident[:, :], in_=ident[:, :], compare_op=ALU.not_equal, fill=1.0,
                                     base=0, pattern=[[-1, P]], channel_multiplier=1))
            const(pool.affine_select(out=causal[:, :], in_=causal[:, :], compare_op=ALU.is_ge, fill=0.0,
                                     base=0, pattern=[[1, P]], channel_multiplier=-1))
            const(pool.affine_select(out=before[:, :], in_=before[:, :], compare_op=ALU.is_ge, fill=0.0,
                                     base=-1, pattern=[[1, P]], channel_multiplier=-1))
            def count_up(ap, pattern, base, channel):
                const(pool.iota(ap, pattern=pattern, base=base, channel_multiplier=channel,
                                allow_small_or_imprecise_dtypes=True))

            count_up(pad_row[:, ROW - 1:ROW], [[1, 1]], TOP * N, 1)
            for h in range(HEADS):
                const(pool.memset(head_pick[h * dk:(h + 1) * dk, h:h + 1], 1.0))
            for c in range(P // dv):
                const(pool.memset(block_ones[c * dv:(c + 1) * dv, c * dv:(c + 1) * dv], 1.0))

            count_up(expert_id[:, :], [[1, E]], 0, 0)
            count_up(expert_row[:, :], [[CAP, E]], 0, 0)
            count_up(full_tiles[:, :, :], [[0, E], [P, T]], 0, 0)
            count_up(slot_id[:, :], [[1, SLOTS]], 0, 0)
            count_up(xr[:, :, :, ROW - 1], [[TOP * P, T], [1, TOP]], 0, TOP)
            def scale_k(g):
                c = slice(g * GROUP, (g + 1) * GROUP)
                t = slice(g * TG, (g + 1) * TG)
                pool.wait_ge(s_eq, 2 * (g + 1))
                pool.tensor_tensor(km[:, c], kT[:, c], ek[:, g % 2, :], ALU.mult).then_inc(s_km, 1)
                pool.wait_ge(s_km, g + 1)
                pool.tensor_tensor(tiles(kc[:, c]), tiles(km[:, c]), wide(er[:, t], P), ALU.mult).then_inc(s_kc, 1)

            scale_k(0)

            def gate_over_rms(t):
                pool.wait_ge(s_rr, t + 1)
                if t >= 2:
                    pool.wait_ge(s_og, t - 1)
                pool.tensor_tensor(rgate[:, t % 2, :, :], rrms[:, t % 2, :, :], gate[:, :, t * P:(t + 1) * P],
                                   ALU.mult).then_inc(s_rg, 1)

            def scatter_rows(t):
                for k in range(TOP):
                    pool.indirect_dma_start(out=rows[:, :], in_=xr[:, t, k, :], in_offset=None,
                                            out_offset=bass.IndirectOffsetOnAxis(ap=slot[:, t, k:k + 1], axis=0)
                                            ).then_inc(s_scat, 16)

            pool.wait_ge(s_pad, 16 * E)
            pool.wait_ge(s_jact, n_act)
            for i in range(ROUNDS + 2):
                t = at_age(i, AGE_GATE)
                if t is not None:
                    gate_over_rms(t)
                if i in groups_ended:
                    scale_k(groups_ended[i])
                b = batch_at(i, AGE_PLACE + 1)
                if b is not None:
                    pool.wait_ge(s_slot, b + 1)
                    pool.wait_ge(s_weight, b + 1)
                    pool.wait_ge(s_xcopy, 2 * (b + 1))
                    scatter_rows(2 * b)
                b = batch_at(i, AGE_PLACE + 2)
                if b is not None:
                    scatter_rows(2 * b + 1)

            def scatter_results(i, u, peeled):
                pool.wait_ge(s_xg[i % AHEAD], (i // AHEAD + 1) * 16)
                if not peeled or i >= 3:
                    pool.wait_ge(s_out[u], (i // 3) * 16)
                pool.tensor_copy(dest[:, u:u + 1], xg[:, i % AHEAD, ROW - 1:ROW]).then_inc(s_dest, 1)
                pool.wait_ge(s_dest, i + 1)
                pool.wait_ge(s_yw, i + 1)
                pool.indirect_dma_start(out=results[:, :], in_=yw[:, u, :], in_offset=None,
                                        bounds_check=TOP * N - 1, oob_is_err=False,
                                        out_offset=bass.IndirectOffsetOnAxis(ap=dest[:, u:u + 1], axis=0)
                                        ).then_inc(s_out[u], 16)

            for i in range(SLOTS):
                scatter_results(i, i % 3, True)
            for g in range(NG):
                t = slice(g * TG, (g + 1) * TG)
                pool.wait_ge(s_ysum[g], 16)
                pool.tensor_tensor(acc[:, t, :], ysum[:, t, 0:D], xr[:, t, 0, 0:D], ALU.add).then_inc(s_acc0, 1)

        @block.scalar
        def _(act):
            act.dma_start(wgk1_sb[:, :], Wgk1).then_inc(s_gatew, 16)
            act.dma_start(wgk2_sb[:, :], Wgk2).then_inc(s_gatew, 16)
            act.dma_start(bgk2_sb[:, :], bgk2.rearrange("(p a) -> p a", a=1)).then_inc(s_gatew, 16)
            act.dma_start(wq_sb[:, :], Wq).then_inc(s_projw, 16)
            act.dma_start(wk_sb[:, :], Wk).then_inc(s_projw, 16)
            act.dma_start(wr_sb[:, :], Wr).then_inc(s_router, 16)
            act.dma_start(br_sb[:, :], br.partition_broadcast(P)).then_inc(s_router, 16)
            act.dma_start(b1_in[:, :], b1.rearrange("e (j p) -> (e j) p", p=P)).then_inc(s_b1, 16)
            act.preload_act_table_set("natural_log_exp_and_others")

            def softplus(g):
                c = slice(g * GROUP, (g + 1) * GROUP)
                act.wait_ge(s_jdve, emptied(at["z", g])[1])
                act.activation(soft[:, c], zb[:, c], ACT.Abs).then_inc(s_abs, 1)
                act.wait_ge(s_abs, g + 1)
                act.activation(soft[:, c], soft[:, c], ACT.Exp, scale=-1.0).then_inc(s_exp, 1)
                act.wait_ge(s_exp, g + 1)
                act.activation(soft[:, c], soft[:, c], ACT.Ln, bias=1.0).then_inc(s_soft, 1)

            def take_qk(g):
                c = slice(g * GROUP, (g + 1) * GROUP)
                act.wait_ge(s_job, at["q", g] + 1)
                act.activation(qT[:, c], bank_of("q", g)[:, :], ACT.Copy, scale=float(dk) ** -0.5).then_inc(s_jact, 1)
                act.wait_ge(s_job, at["k", g] + 1)
                act.activation(kT[:, c], bank_of("k", g)[:, :], ACT.Copy).then_inc(s_jact, 1)

            def factors(g):
                if g == 0:
                    act.wait_ge(s_cum, NG)
                    act.wait_ge(s_rest, NG)
                    ct = tiles(cum[:, :])
                    act.activation(em[:, :], ct[:, :, MID], ACT.Exp, scale=1 / GATE_NORMALIZER).then_inc(s_small, 1)
                    act.activation(er[:, :], rest[:, :], ACT.Exp, scale=1 / GATE_NORMALIZER).then_inc(s_small, 1)
                    act.activation(tile_decay[:, :], ct[:, :, P - 1], ACT.Exp, scale=1 / GATE_NORMALIZER).then_inc(s_small, 1)
                act.wait_ge(s_dist, g + 1)
                if g >= 2:
                    act.wait_ge(s_qm, g - 1)
                    act.wait_ge(s_km, g - 1)
                act.activation(eq[:, g % 2, :], dist[:, g % 2, :], ACT.Exp, scale=1 / GATE_NORMALIZER).then_inc(s_eq, 1)
                act.activation(ek[:, g % 2, :], dist[:, g % 2, :], ACT.Exp, scale=-1 / GATE_NORMALIZER).then_inc(s_eq, 1)

            act.wait_ge(s_dinit, 8)
            for g in range(1, NG, 2):
                act.wait_ge(s_job, at["xT", g] + 1)
                act.activation(xT[:, g * GROUP:(g + 1) * GROUP], bank_of("xT", g), ACT.Copy).then_inc(s_jact, 1)
            for g in range(NG):
                softplus(g)
                take_qk(g)
            factors(0)
            for g in range(2 * NG):
                act.wait_ge(s_job, at["g", g] + 1)
                act.activation(gate[:, g % DVC, g // DVC * GROUP:(g // DVC + 1) * GROUP], bank_of("g", g),
                               ACT.Silu).then_inc(s_jact, 1)

            act.wait_ge(s_flag, 1)
            too_wide = act.value_load(wide_flag[0:1, 0:1], min_val=0, max_val=1)
            with act.If(too_wide):
                act.wait_ge(s_qc, 1)
                act.wait_ge(s_kc, 1)
                act.preload_act_table_set("natural_log_exp_and_others")
                act.activation(decay[:, :], gT[:, :], ACT.Exp, scale=1 / GATE_NORMALIZER).then_inc(s_turn, 1)

            act.preload_act_table_set("natural_log_exp_and_others")

            def inverse_rms(t):
                act.activation(lrms[:, :, :], bank[6][:, 256:512].rearrange("p (c t) -> p c t", t=P), ACT.Ln,
                               bias=eps_sb[:, :], scale=1.0 / dv).then_inc(s_lrms, 1)
                act.wait_ge(s_lrms, t + 1)
                if t >= 2:
                    act.wait_ge(s_rg, t - 1)
                act.activation(rrms[:, t % 2, :, :], lrms[:, :, :], ACT.Exp, scale=-0.5).then_inc(s_rr, 1)

            def copy_kcT(t):
                act.activation(kcT[:, t % 2, :], bank[6][:, 0:P], ACT.Copy).then_inc(s_kcT, 1)

            def copy_x1T(t):
                if t >= 2:
                    act.wait_ge(s_dve_bank, t - 2 + AGE_ROUTE)
                act.activation(x1T[:, t % 2, :], bank[6][:, P:2 * P], ACT.Copy).then_inc(s_x1T, 1)

            def copy_row(t):
                act.wait_ge(s_x1, t + 1)
                act.activation(xr[:, t, 1, 0:D], xr[:, t, 0, 0:D], ACT.Copy).then_inc(s_xcopy, 1)

            def inverse_std(t):
                b = t % 2
                act.wait_ge(s_mv, t + 1)
                act.activation(lstd[:, b, :], mv[:, b, 1:2], ACT.Ln, bias=eps_sb[:, :]).then_inc(s_lstd, 1)
                act.wait_ge(s_lstd, t + 1)
                if t >= 2:
                    act.wait_ge(s_x1, t - 1)
                act.activation(rstd[:, b, :], lstd[:, b, :], ACT.Exp, scale=-0.5).then_inc(s_rstd, 1)

            def square_o(t):
                act.wait_ge(s_o, t + 1)
                act.activation(sq[:, t % 2, :, :], bank[4 + t % 2][:, 0:DV].rearrange("p (c t) -> p c t", t=P),
                               ACT.Square).then_inc(s_sq, 1)

            def exp_gap(b):
                act.wait_ge(s_gap, b + 1)
                act.activation(egap[:, 2 * b:2 * b + 2], gap[:, 2 * b:2 * b + 2], ACT.Exp).then_inc(s_egap, 1)

            for i in range(ROUNDS):
                if i <= T - 1 + AGE_X1T:
                    act.wait_ge(s_act_bank, i + 1)
                for age, stage in ((AGE_GATE, inverse_rms), (0, copy_kcT), (AGE_X1T, copy_x1T), (AGE_X1T, copy_row)):
                    t = at_age(i, age)
                    if t is not None:
                        stage(t)
                b = batch_at(i, AGE_PLACE)
                if b is not None:
                    exp_gap(b)
                for age, stage in ((AGE_OUT, inverse_std), (AGE_O, square_o)):
                    t = at_age(i, age)
                    if t is not None:
                        stage(t)
                if i in groups_begun:
                    factors(groups_begun[i])

            act.wait_ge(s_table, 1)

            def copy_rows(i, u, peeled):
                act.wait_ge(s_gt, i + 1)
                if not peeled or i >= 3:
                    act.wait_ge(s_hb, i - 2)
                act.activation(xgT[:, u, :], bank[7][:, 0:P], ACT.Copy).then_inc(s_gT, 1)

            def hidden_lower(i, u, peeled):
                e = act.value_load(table[0:1, 0, i:i + 1] if peeled else table[0:1, 0, bass.ds(i, 1)], min_val=0, max_val=E - 1)
                act.wait_ge(s_ha, i + 1)
                if not peeled or i >= 3:
                    act.wait_ge(s_ye, i - 2)
                for j in range(HC // 2):
                    act.activation(hT[:, u, j, :], bank[2 * u][:, j * P:(j + 1) * P], ACT.Relu,
                                   bias=b1_sb[:, bass.ds(e * HC + j, 1)]).then_inc(s_hTa, 1)

            copy_rows(0, 0, True)
            copy_rows(1, 1, True)
            for i in range(SLOTS):
                hidden_lower(i, i % 3, True)
                if i + 2 < SLOTS:
                    copy_rows(i + 2, (i + 2) % 3, True)
            for g in range(NG):
                t = slice(g * TG, (g + 1) * TG)
                act.wait_ge(s_fmv, (g + 1) * TG)
                act.activation(flog[:, t], fmv[:, t, 1], ACT.Ln, bias=eps_sb[:, :]).then_inc(s_flog, 1)
                act.wait_ge(s_flog, g + 1)
                act.activation(frstd[:, t], flog[:, t], ACT.Exp, scale=-0.5).then_inc(s_frs, 1)
                act.wait_ge(s_frs, g + 1)
                act.wait_ge(s_fshift, g + 1)
                for n in range(g * TG, (g + 1) * TG):
                    act.activation(result[:, n, :], acc[:, n, :], ACT.Identity, bias=fshift[:, n:n + 1],
                                   scale=frstd[:, n:n + 1]).then_inc(s_result, 1)

        @block.vector
        def _(dve):
            dve.memset(seg[:, :], 1.0).then_inc(s_dinit, 1)
            dve.memset(ones[:, :], 1.0).then_inc(s_dinit, 1)
            dve.memset(aT[:, :, :, :], 0.0).then_inc(s_dinit, 1)
            dve.memset(eps_sb[:, :], EPS).then_inc(s_dinit, 1)
            dve.memset(so_far[:, 0, :], 0.0).then_inc(s_dinit, 1)
            dve.memset(state[:, :, :], 0.0).then_inc(s_dinit, 1)
            dve.wait_ge(s_dinit, 6)
            dve.memset(seg[:, 0::P], 0.0).then_inc(s_dinit, 1)
            dve.wait_ge(s_const, 2)
            dve.tensor_copy(keep[:, :], causal[:, :]).then_inc(s_dinit, 1)

            def take_xT(g):
                dve.wait_ge(s_job, at["xT", g] + 1)
                dve.tensor_copy(xT[:, g * GROUP:(g + 1) * GROUP], bank_of("xT", g)).then_inc(s_jdve, 1)

            def take_z(g):
                dve.wait_ge(s_job, at["z", g] + 1)
                if g == 0:
                    dve.wait_ge(s_gatew, 48)
                dve.tensor_scalar(zb[:, g * GROUP:(g + 1) * GROUP], bank_of("z", g), bgk2_sb[:, 0:1], None,
                                  ALU.add).then_inc(s_jdve, 1)

            take_xT(0)
            dve.wait_ge(s_job, at["wgk1T", 0] + 1)
            dve.tensor_copy(wgk1T[:, :], bank_of("wgk1T", 0)[0:R, 0:P]).then_inc(s_jdve, 1)
            dve.wait_ge(s_job, at["wgk", 0] + 1)
            dve.tensor_copy(wgk[:, :], bank_of("wgk", 0)[:, 0:P]).then_inc(s_jdve, 1)
            for g in range(1, NG):
                if g % 2 == 0:
                    take_xT(g)
                take_z(g - 1)
            take_z(NG - 1)

            def take_v(g):
                dve.wait_ge(s_job, at["v", g] + 1)
                dve.tensor_copy(v_sb[:, 2 * g:2 * g + 2, :], bank_of("v", g).rearrange("p (t v) -> p t v", v=DV)).then_inc(s_jdve, 1)

            def log_decays(g):
                c = slice(g * GROUP, (g + 1) * GROUP)
                t = slice(g * TG, (g + 1) * TG)
                cg = tiles(cum[:, c])
                dve.wait_ge(s_soft, g + 1)
                dve.wait_ge(s_jdve, emptied(at["z", g])[1])
                dve.scalar_tensor_tensor(gT[:, c], zb[:, c], 0.0, soft[:, c], ALU.min, ALU.subtract).then_inc(s_g, 1)
                dve.wait_ge(s_g, g + 1)
                if g == 0:
                    dve.wait_ge(s_dinit, 8)
                dve.tensor_tensor_scan(cum[:, c], seg[:, :], gT[:, c], 0.0, ALU.mult, ALU.add).then_inc(s_cum, 1)
                dve.wait_ge(s_cum, g + 1)
                dve.tensor_tensor(rest[:, t], cg[:, :, P - 1], cg[:, :, MID], ALU.subtract).then_inc(s_rest, 1)
                dve.tensor_tensor(span[:, 0, t], cg[:, :, 0], cg[:, :, MID], ALU.subtract).then_inc(s_span, 1)
                dve.tensor_tensor(span[:, 1, t], cg[:, :, MID], cg[:, :, P - 1], ALU.subtract).then_inc(s_span, 1)

            def distances(g):
                cg = tiles(cum[:, g * GROUP:(g + 1) * GROUP])
                if g >= 2:
                    dve.wait_ge(s_eq, 2 * (g - 1))
                dve.tensor_tensor(tiles(dist[:, g % 2, :]), cg, wide(cg[:, :, MID], P), ALU.subtract).then_inc(s_dist0, 1)
                dve.wait_ge(s_dist0, g + 1)
                dve.tensor_scalar(dist[:, g % 2, :], dist[:, g % 2, :], SAFE * GATE_NORMALIZER, -SAFE * GATE_NORMALIZER,
                                  ALU.min, ALU.max).then_inc(s_dist, 1)

            def scale_q(g):
                c = slice(g * GROUP, (g + 1) * GROUP)
                t = slice(g * TG, (g + 1) * TG)
                dve.wait_ge(s_eq, 2 * g + 1)
                if g == 0:
                    dve.wait_ge(s_jact, emptied(at["k", NG - 1])[1])
                dve.tensor_tensor(qm[:, c], qT[:, c], eq[:, g % 2, :], ALU.mult).then_inc(s_qm, 1)
                dve.wait_ge(s_qm, g + 1)
                dve.tensor_tensor(tiles(qc[:, c]), tiles(qm[:, c]), wide(em[:, t], P), ALU.mult).then_inc(s_qc, 1)

            for g in range(NG):
                log_decays(g)
                if g == 0:
                    distances(0)
                take_v(2 * g)
                take_v(2 * g + 1)
            scale_q(0)
            dve.wait_ge(s_span, 2 * NG)
            dve.tensor_reduce(widest[:, :], span[:, :, :].rearrange("p a n -> p (a n)"), AX_X, ALU.max).then_inc(s_widest, 1)
            dve.wait_ge(s_job, at["b1T", 0] + 1)
            dve.tensor_copy(b1_sb[:, :], bank_of("b1T", 0)[:, 0:E * HC]).then_inc(s_jdve, 1)
            dve.wait_ge(s_job, at["span", 0] + 1)
            dve.tensor_reduce(worst[:, :], bank_of("span", 0)[0:1, 0:P], AX_X, ALU.max).then_inc(s_jdve, 1)
            dve.wait_ge(s_jdve, n_dve)
            dve.tensor_scalar(wide_flag[:, :], worst[:, :], SAFE * GATE_NORMALIZER, None, ALU.is_gt).then_inc(s_flag, 1)

            dve.wait_ge(s_wo, 16 * (1 + P // dv))
            dve.tensor_scalar(wo_sb[:, :, :], wo_in[:, :, :], gnorm_sb[:, 0:1], None, ALU.mult).then_inc(s_wo2, 1)

            dve.wait_ge(s_flag, 1)
            too_wide = dve.value_load(wide_flag[0:1, 0:1], min_val=0, max_val=1)
            with dve.If(too_wide):
                with dve.Fori(0, dv) as v:
                    turn = v * V_STEPS + 1
                    dve.wait_ge(s_turn, turn)
                    dve.tensor_scalar(v_col, v_heads[:, :, :, bass.ds(v, 1)].to_broadcast([P, T, HEADS, dk]),
                                      1.0, None, ALU.mult).then_inc(s_turn, 1)
                    for g in range(NG):
                        c = slice(g * GROUP, (g + 1) * GROUP)
                        dve.wait_ge(s_turn, turn + 2 + g)
                        dve.tensor_tensor(outer[:, c], kT[:, c], bank[g], ALU.mult).then_inc(s_turn, 1)
                    dve.wait_ge(s_turn, turn + 2 + NG)
                    dve.tensor_tensor_scan(states[:, :], decay[:, :], outer[:, :], 0.0, ALU.mult, ALU.add).then_inc(s_turn, 1)
                    for g in range(NG):
                        c = slice(g * GROUP, (g + 1) * GROUP)
                        dve.wait_ge(s_turn, turn + 3 + NG + g)
                        dve.tensor_tensor(q_states[:, c], qT[:, c], states[:, c], ALU.mult).then_inc(s_turn, 1)
                    dve.wait_ge(s_turn, turn + 4 + 2 * NG)
                    dve.tensor_scalar(v_heads[:, :, :, bass.ds(v, 1)].rearrange("p t h a -> p t (h a)"),
                                      bank[4][:, 0:T * HEADS].rearrange("p (t h) -> p t h", h=HEADS),
                                      1.0, None, ALU.mult).then_inc(s_turn, 1)
                dve.wait_ge(s_turn, V_END)
                dve.memset(qT[:, :], 1.0 / dk).then_inc(s_turn, 1)
                dve.memset(kT[:, :], 1.0).then_inc(s_turn, 1)
                dve.memset(cum[:, :], 0.0).then_inc(s_turn, 1)
                dve.memset(er[:, :], 0.0).then_inc(s_turn, 1)
                dve.memset(qm[:, 0:GROUP], 1.0 / dk).then_inc(s_turn, 1)
                dve.memset(km[:, 0:GROUP], 1.0).then_inc(s_turn, 1)
                dve.memset(kc[:, 0:GROUP], 0.0).then_inc(s_turn, 1)
                dve.tensor_copy(keep[:, :], ident[:, :]).then_inc(s_turn, 1)
                dve.wait_ge(s_turn, V_END + 8)

            def mask_scores(t):
                dve.wait_ge(s_a, t + 1)
                if t >= 2:
                    dve.wait_ge(s_o, t - 1)
                dve.copy_predicated(aT[:, t % 2, :, :], keep[:, :].unsqueeze(1).to_broadcast([P, HEADS, P]),
                                    psum[:, 0:HEADS, 0:P]).then_inc(s_aT, 1)

            def residual(t):
                dve.tensor_tensor(res[:, t % 2, :], bank[7][:, 256:256 + D], x_sb[:, t, :], ALU.add).then_inc(s_res, 1)

            def update_state(t):
                if t >= 2:
                    dve.wait_ge(s_o, t)
                if t:
                    dve.wait_ge(s_state, HEADS * t)
                for h in range(HEADS):
                    r = slice(h * dk, (h + 1) * dk)
                    v = slice(h * dv, (h + 1) * dv)
                    if t == 0:
                        ins = dve.tensor_copy(state[r, 0, v], bank[7][r, v])
                    else:
                        ins = dve.scalar_tensor_tensor(state[r, t % 2, v], state[r, (t - 1) % 2, v], tile_decay[r, t:t + 1],
                                                       bank[7][r, v], ALU.mult, ALU.add)
                    ins.then_inc(s_state, 1)

            def take_score(t):
                dve.tensor_tensor(score[:, t, :], bank[7][:, 384:384 + E], br_sb[:, :], ALU.add).then_inc(s_score, 1)

            def mean_var(t):
                b = t % 2
                dve.wait_ge(s_res, t + 1)
                dve.bn_stats(stats[:, b, :], res[:, b, :]).then_inc(s_st, 1)
                dve.wait_ge(s_st, t + 1)
                if t >= 2:
                    dve.wait_ge(s_x1, t - 1)
                dve.bn_aggr(mv[:, b, :], stats[:, b, :]).then_inc(s_mv, 1)

            def gate_o(t):
                dve.wait_ge(s_rg, t + 1)
                dve.tensor_tensor(ogT[:, t % 2, :, :], bank[4 + t % 2][:, 0:DV].rearrange("p (c t) -> p c t", t=P),
                                  rgate[:, t % 2, :, :], ALU.mult).then_inc(s_og, 1)

            def normalize(t):
                b = t % 2
                dve.wait_ge(s_rstd, t + 1)
                dve.tensor_scalar(xr[:, t, 0, 0:D], res[:, b, :], mv[:, b, 0:1], rstd[:, b, :],
                                  ALU.subtract, ALU.mult).then_inc(s_x1, 1)

            def choose(b):
                tt = slice(2 * b, 2 * b + 2)
                dve.wait_ge(s_score, 2 * b + 2)
                for t in (2 * b, 2 * b + 1):
                    dve.max(top8[:, t, :], score[:, t, :]).then_inc(s_top, 1)
                for t in (2 * b, 2 * b + 1):
                    dve.wait_ge(s_top, t + 1)
                    dve.max_index(top_at[:, t, :], top8[:, t, :], score[:, t, :]).then_inc(s_topat, 1)
                dve.tensor_tensor(gap[:, tt], top8[:, tt, 1], top8[:, tt, 0], ALU.subtract).then_inc(s_gap, 1)
                dve.wait_ge(s_topat, 2 * b + 2)
                dve.tensor_copy(top_f[:, tt, :], top_at[:, tt, 0:TOP]).then_inc(s_topf, 1)
                dve.wait_ge(s_topf, b + 1)
                for t in (2 * b, 2 * b + 1):
                    dve.tensor_tensor(hot[:, t, :, :], expert_id[:, :].unsqueeze(1).to_broadcast([P, TOP, E]),
                                      wide(top_f[:, t, :], E), ALU.is_equal).then_inc(s_hot, 1)
                dve.wait_ge(s_hot, 2 * b + 2)
                dve.tensor_tensor(hit[:, tt, :], hot[:, tt, 0, :], hot[:, tt, 1, :], ALU.add).then_inc(s_hit, 1)
                for t in (2 * b, 2 * b + 1):
                    dve.wait_ge(s_hit, b + 1)
                    if t:
                        dve.wait_ge(s_sofar, t)
                    dve.tensor_tensor(so_far[:, t + 1, :], so_far[:, t, :], hit[:, t, :], ALU.add).then_inc(s_sofar, 1)

            def weigh(b):
                tt = slice(2 * b, 2 * b + 2)
                dve.wait_ge(s_egap, b + 1)
                dve.tensor_scalar(wsum[:, tt], egap[:, tt], 1.0, None, ALU.add).then_inc(s_wsum, 1)
                dve.wait_ge(s_wsum, b + 1)
                dve.reciprocal(xr[:, tt, 0, D], wsum[:, tt]).then_inc(s_w1st, 1)
                dve.wait_ge(s_w1st, b + 1)
                dve.tensor_tensor(xr[:, tt, 1, D], egap[:, tt], xr[:, tt, 0, D], ALU.mult).then_inc(s_weight, 1)

            def take_places(b):
                tt = slice(2 * b, 2 * b + 2)
                dve.tensor_tensor(place[:, tt, :], bank[7][:, 400:400 + 2 * E].rearrange("p (t e) -> p t e", e=E),
                                  expert_row[:, :].unsqueeze(1).to_broadcast([P, 2, E]), ALU.add).then_inc(s_place0, 1)

            def find_slots(b):
                tt = slice(2 * b, 2 * b + 2)
                dve.wait_ge(s_place0, b + 1)
                for k in range(TOP):
                    dve.tensor_tensor(placed[:, tt, k, :], hot[:, tt, k, :], place[:, tt, :], ALU.mult).then_inc(s_placed, 1)
                dve.wait_ge(s_placed, TOP * (b + 1))
                dve.tensor_reduce(slot_f[:, tt, :], placed[:, tt, :, :], AX_X, ALU.add).then_inc(s_slotf, 1)
                dve.wait_ge(s_slotf, b + 1)
                dve.tensor_copy(slot[:, tt, :], slot_f[:, tt, :]).then_inc(s_slot, 1)

            dve.wait_ge(s_router, 32)
            dve.wait_ge(s_const, 15)
            for i in range(ROUNDS + 1):
                b = batch_at(i, AGE_PLACE)
                if b is not None:
                    choose(b)
                if i < T:
                    mask_scores(i)
                before_that = batch_at(i, AGE_PLACE + 1)
                if before_that is not None:
                    weigh(before_that)
                    find_slots(before_that)
                if 0 < i < ROUNDS:
                    dve.wait_ge(s_dve_bank, i)
                for age, stage in ((AGE_OUT, residual), (AGE_OUT, mean_var), (AGE_O, update_state), (AGE_ROUTE, take_score)):
                    t = at_age(i, age)
                    if t is not None:
                        stage(t)
                if b is not None:
                    take_places(b)
                if i == ROUNDS - 1:
                    dve.tensor_copy(count[:, :], bank[7][0:1, 432:432 + E]).then_inc(s_tab, 1)
                for age, stage in ((AGE_GATE, gate_o), (AGE_OUT, normalize)):
                    t = at_age(i, age)
                    if t is not None:
                        stage(t)
                if i in groups_begun:
                    distances(groups_begun[i])
                if i in groups_ended:
                    scale_q(groups_ended[i])

            step = [1]

            def chain(ins):
                step[0] += 1
                ins.then_inc(s_tab, 1)
                dve.wait_ge(s_tab, step[0])

            dve.wait_ge(s_tab, 1)
            chain(dve.tensor_tensor(more[:, :, :], wide(count[:, :], T), full_tiles[:, :, :], ALU.is_gt))
            chain(dve.tensor_reduce(ntile[:, :], more[:, :, :], AX_X, ALU.add))
            chain(dve.tensor_tensor_scan(ends[:, :], ones[0:1, 0:E], ntile[:, :], 0.0, ALU.mult, ALU.add))
            by_slot = lambda a: a[:, :].unsqueeze(1).to_broadcast([1, SLOTS, E])
            chain(dve.tensor_tensor(past[:, :, :], wide(slot_id[:, :], E), by_slot(ends), ALU.is_ge))
            chain(dve.tensor_reduce(slot_e[:, :], past[:, :, :], AX_X, ALU.add))
            chain(dve.tensor_tensor(past_tiles[:, :, :], past[:, :, :], by_slot(ntile), ALU.mult))
            chain(dve.tensor_reduce(slot_t[:, :], past_tiles[:, :, :], AX_X, ALU.add))
            chain(dve.tensor_tensor(slot_t[:, :], slot_id[:, :], slot_t[:, :], ALU.subtract))
            chain(dve.tensor_scalar(slot_t[:, :], slot_t[:, :], float(P), None, ALU.mult))
            chain(dve.scalar_tensor_tensor(slot_row[:, :], slot_e[:, :], float(CAP), slot_t[:, :], ALU.mult, ALU.add))
            chain(dve.tensor_scalar(used[:, :], slot_e[:, :], float(E), None, ALU.is_lt))
            chain(dve.tensor_tensor(slot_table[:, 0, :], slot_e[:, :], used[:, :], ALU.mult))
            chain(dve.tensor_tensor(slot_row[:, :], slot_row[:, :], used[:, :], ALU.mult))
            chain(dve.tensor_scalar(used[:, :], used[:, :], -float(CAP - P), float(CAP - P), ALU.mult, ALU.add))
            chain(dve.tensor_tensor(slot_table[:, 1, :], slot_row[:, :], used[:, :], ALU.add))
            dve.tensor_copy(table[:, :, :], slot_table[:, :, :]).then_inc(s_table, 1)
            dve.wait_ge(s_table, 1)

            def hidden_upper(i, u, peeled):
                e = dve.value_load(table[0:1, 0, i:i + 1] if peeled else table[0:1, 0, bass.ds(i, 1)], min_val=0, max_val=E - 1)
                dve.wait_ge(s_hb, i + 1)
                if not peeled or i >= 3:
                    dve.wait_ge(s_ye, i - 2)
                for j in range(HC // 2, HC):
                    dve.tensor_scalar(hT[:, u, j, :], bank[2 * u + 1][:, (j - HC // 2) * P:(j - HC // 2 + 1) * P],
                                      b1_sb[:, bass.ds(e * HC + j, 1)], 0.0, ALU.add, ALU.max).then_inc(s_hTb, 1)
                return e

            def weighted(i, u, e, peeled):
                dve.wait_ge(s_ye, i + 1)
                dve.tensor_tensor(yb[:, u, :], bank[6][:, 0:D], b2_sb[:, bass.ds(e, 1), :].rearrange("p a d -> p (a d)"),
                                  ALU.add).then_inc(s_yb, 1)
                dve.wait_ge(s_yb, i + 1)
                if not peeled or i >= 3:
                    dve.wait_ge(s_out[u], (i // 3) * 16)
                dve.tensor_scalar(yw[:, u, :], yb[:, u, :], xg[:, i % AHEAD, D:D + 1], None, ALU.mult).then_inc(s_yw, 1)

            dve.wait_ge(s_w2, 32)
            es = {0: hidden_upper(0, 0, True)}
            for i in range(SLOTS):
                if i + 1 < SLOTS:
                    es[i + 1] = hidden_upper(i + 1, (i + 1) % 3, True)
                weighted(i, i % 3, es.pop(i), True)

            for g in range(NG):
                t = slice(g * TG, (g + 1) * TG)
                dve.wait_ge(s_acc0, g + 1)
                dve.tensor_tensor(acc[:, t, :], acc[:, t, :], ysum[:, t, D:2 * D], ALU.add).then_inc(s_acc, 1)
                dve.wait_ge(s_acc, g + 1)
                for n in range(g * TG, (g + 1) * TG):
                    dve.bn_stats(fstats[:, n, :], acc[:, n, :]).then_inc(s_fst, 1)
                for n in range(g * TG, (g + 1) * TG):
                    dve.wait_ge(s_fst, n + 1)
                    dve.bn_aggr(fmv[:, n, :], fstats[:, n, :]).then_inc(s_fmv, 1)
                dve.wait_ge(s_fmv, (g + 1) * TG)
                dve.wait_ge(s_frs, g + 1)
                dve.scalar_tensor_tensor(fshift[:, t], fmv[:, t, 0], -1.0, frstd[:, t], ALU.mult, ALU.mult).then_inc(s_fshift, 1)

        @block.tensor
        def _(pe):
            mm = nc.tensor.matmul

            def job(kind, g):
                i = at[kind, g]
                if i >= 8:
                    pe.wait_ge(*emptied(i - 8))
                b = bank[i % 8]
                c = slice(g * GROUP, (g + 1) * GROUP)
                if kind == "xT":
                    pe.wait_ge(s_x[g], 16)
                    if g == 0:
                        pe.wait_ge(s_const, 1)
                    for u in range(TG):
                        last = nc.tensor.transpose(b[:, u * P:(u + 1) * P], x_sb[:, g * TG + u, :], ident[:, :])
                elif kind == "wgk1T":
                    pe.wait_ge(s_gatew, 48)
                    last = nc.tensor.transpose(b[0:R, 0:P], wgk1_sb[:, :], ident[:, :])
                elif kind == "b1T":
                    pe.wait_ge(s_b1, 16)
                    last = nc.tensor.transpose(b[:, 0:E * HC], b1_in[:, :], ident[0:E * HC, 0:E * HC])
                elif kind == "span":
                    pe.wait_ge(s_widest, 1)
                    last = nc.tensor.transpose(b[0:1, 0:P], widest[:, :], ident[:, :])
                elif kind == "wgk":
                    pe.wait_ge(*emptied(at["wgk1T", 0]))
                    last = mm(b[:, 0:P], wgk1T[:, :], wgk2_sb[:, :], start=True, stop=True)
                elif kind == "z":
                    pe.wait_ge(*emptied(at["xT", g]))
                    pe.wait_ge(*emptied(at["wgk", 0]))
                    last = mm(b[:, :], wgk[:, :], xT[:, c], start=True, stop=True)
                elif kind in ("q", "k"):
                    if g == 0:
                        pe.wait_ge(s_projw, 32)
                    last = mm(b[:, :], (wq_sb if kind == "q" else wk_sb)[:, :], xT[:, c], start=True, stop=True)
                elif kind == "v":
                    if g == 0:
                        pe.wait_ge(s_vgw, 32)
                    for u in range(2):
                        t = 2 * g + u
                        last = mm(b[:, u * DV:(u + 1) * DV], xT[:, t * P:(t + 1) * P], wv_sb[:, :], start=True, stop=True)
                else:
                    m, n = g % DVC, g // DVC
                    last = mm(b[:, :], wg_sb[:, m * P:(m + 1) * P], xT[:, n * GROUP:(n + 1) * GROUP], start=True, stop=True)
                last.then_inc(s_job, 1)

            for kind, g, _ in jobs:
                job(kind, g)
            pe.wait_ge(s_jact, n_act)
            pe.wait_ge(s_jdve, n_dve)

            pe.wait_ge(s_flag, 1)
            too_wide = pe.value_load(wide_flag[0:1, 0:1], min_val=0, max_val=1)
            with pe.If(too_wide):
                with pe.Fori(0, dv) as v:
                    turn = v * V_STEPS + 1
                    pe.wait_ge(s_turn, turn + 1)
                    for t in range(T):
                        last = mm(bank[t // TG][:, (t % TG) * P:(t % TG + 1) * P],
                                  v_col[:, t, :, :].rearrange("p h k -> p (h k)"), ident[:, :], start=True, stop=True)
                    last.then_inc(s_turn, 1)
                    pe.wait_ge(s_turn, turn + 3 + 2 * NG)
                    for t in range(T):
                        last = mm(bank[4][:, t * HEADS:(t + 1) * HEADS], q_states[:, t * P:(t + 1) * P], head_pick[:, :],
                                  start=True, stop=True)
                    last.then_inc(s_turn, 1)
                pe.wait_ge(s_turn, V_END + 8)

            def scores(t):
                g = t // TG
                c = slice(t * P, (t + 1) * P)
                if t % TG == 0:
                    pe.wait_ge(s_km, g + 1)
                    pe.wait_ge(s_qc, g + 1)
                    pe.wait_ge(s_kc, g + 1)
                if t:
                    pe.wait_ge(s_aT, t)
                for h in range(HEADS):
                    r = slice(h * dk, (h + 1) * dk)
                    last = mm(bank[h][:, 0:P], km[r, c], qm[r, c], start=True, stop=True)
                last.then_inc(s_a, 1)

            def act_bank_read(i):
                for s, age in ((s_kcT, 0), (s_lrms, AGE_GATE), (s_x1T, AGE_X1T)):
                    t = at_age(i, age)
                    if t is not None:
                        pe.wait_ge(s, t + 1)

            def dve_bank_read(i):
                for s, age, steps in ((s_state, AGE_O, HEADS), (s_res, AGE_OUT, 1), (s_score, AGE_ROUTE, 1)):
                    t = at_age(i, age)
                    if t is not None:
                        pe.wait_ge(s, steps * (t + 1))
                b = batch_at(i, AGE_PLACE)
                if b is not None:
                    pe.wait_ge(s_place0, b + 1)

            def transpose_kc(t):
                return nc.tensor.transpose(bank[6][:, 0:P], kc[:, t * P:(t + 1) * P], ident[:, :])

            def sum_squares(t):
                pe.wait_ge(s_sq, t + 1)
                return mm(bank[6][:, 256:512], block_ones[:, :], sq[:, t % 2, :, :].rearrange("p c t -> p (c t)"),
                          start=True, stop=True)

            def transpose_x1(t):
                pe.wait_ge(s_x1, t + 1)
                return nc.tensor.transpose(bank[6][:, P:2 * P], xr[:, t, 0, 0:D], ident[:, :])

            def update(t):
                pe.wait_ge(s_kcT, t + 1)
                return mm(bank[7][:, 0:DV], kcT[:, t % 2, :], v_sb[:, t, :], start=True, stop=True)

            def project_out(t):
                pe.wait_ge(s_og, t + 1)
                for c in range(DVC):
                    last = mm(bank[7][:, 256:256 + D], ogT[:, t % 2, c, :], wo_sb[:, c, :], start=(c == 0), stop=(c == DVC - 1))
                return last

            def route(t):
                pe.wait_ge(s_x1T, t + 1)
                return mm(bank[7][:, 384:384 + E], x1T[:, t % 2, :], wr_sb[:, :], start=True, stop=True)

            def rank(b):
                pe.wait_ge(s_sofar, 2 * b + 2)
                mm(bank[7][:, 400:400 + 2 * E], before[:, :], hit[:, 2 * b:2 * b + 2, :].rearrange("p t e -> p (t e)"),
                   start=True, stop=False)
                return mm(bank[7][:, 400:400 + 2 * E], ones[:, :], so_far[:, 2 * b:2 * b + 2, :].rearrange("p t e -> p (t e)"),
                          start=False, stop=True)

            def attend(t):
                b = bank[4 + t % 2]
                pe.wait_ge(s_aT, t + 1)
                if t >= 2:
                    pe.wait_ge(s_og, t - 1)
                if t:
                    pe.wait_ge(s_state, HEADS * t)
                    for c in range(DVC):
                        mm(b[:, c * P:(c + 1) * P], state[:, (t - 1) % 2, c * P:(c + 1) * P], qc[:, t * P:(t + 1) * P],
                           start=(c == 0), stop=True, skip_group_check=True)
                for h in range(HEADS):
                    c, r = h // DVC, (h % DVC) * dv
                    last = mm(b[r:r + dv, c * P:(c + 1) * P], v_sb[:, t, h * dv:(h + 1) * dv], aT[:, t % 2, h, :],
                              start=(t == 0 and c == 0), stop=True, skip_group_check=True)
                last.then_inc(s_o, 1)

            pe.wait_ge(s_wo2, 1)
            pe.wait_ge(s_router, 32)
            for i in range(ROUNDS):
                if i < T:
                    scores(i)
                if i <= T - 1 + AGE_X1T:
                    if i:
                        act_bank_read(i - 1)
                    for age, stage in ((0, transpose_kc), (AGE_GATE, sum_squares), (AGE_X1T, transpose_x1)):
                        t = at_age(i, age)
                        if t is not None:
                            last = stage(t)
                    last.then_inc(s_act_bank, 1)
                if i:
                    dve_bank_read(i - 1)
                    for age, stage in ((AGE_O, update), (AGE_OUT, project_out), (AGE_ROUTE, route)):
                        t = at_age(i, age)
                        if t is not None:
                            last = stage(t)
                    b = batch_at(i, AGE_PLACE)
                    if b is not None:
                        last = rank(b)
                    if i == ROUNDS - 1:
                        last = mm(bank[7][:, 432:432 + E], ones[:, :], so_far[:, T, :], start=True, stop=True)
                    last.then_inc(s_dve_bank, 1)
                if at_age(i, AGE_O) is not None:
                    attend(i - AGE_O)

            pe.wait_ge(s_table, 1)
            pe.wait_ge(s_w2, 32)

            def transpose_rows(i, u, peeled):
                pe.wait_ge(s_xg[i % AHEAD], (i // AHEAD + 1) * 16)
                if not peeled or i >= 1:
                    pe.wait_ge(s_gT, i)
                nc.tensor.transpose(bank[7][:, 0:P], xg[:, i % AHEAD, 0:D], ident[:, :]).then_inc(s_gt, 1)

            def hidden(i, u, peeled):
                pe.wait_ge(s_gT, i + 1)
                pe.wait_ge(s_w1[i % AHEAD], (i // AHEAD + 1) * 16)
                if not peeled or i >= 3:
                    pe.wait_ge(s_hTa, (i - 2) * (HC // 2))
                    pe.wait_ge(s_hTb, (i - 2) * (HC // 2))
                for half, s in ((0, s_ha), (1, s_hb)):
                    for j in range(HC // 2):
                        n = half * (HC // 2) + j
                        last = mm(bank[2 * u + half][:, j * P:(j + 1) * P], w1_buf[i % AHEAD][:, n * P:(n + 1) * P], xgT[:, u, :],
                                  start=True, stop=True)
                    last.then_inc(s, 1)

            def expert_out(i, u, e, peeled):
                pe.wait_ge(s_hTa, (i + 1) * (HC // 2))
                pe.wait_ge(s_hTb, (i + 1) * (HC // 2))
                if not peeled or i >= 1:
                    pe.wait_ge(s_yb, i)
                for j in range(HC):
                    last = mm(bank[6][:, 0:D], hT[:, u, j, :], w2_sb[:, bass.ds(e, 1), j * D:(j + 1) * D].rearrange("p a d -> p (a d)"),
                              start=(j == 0), stop=(j == HC - 1))
                last.then_inc(s_ye, 1)

            def expert_of(i, peeled):
                return pe.value_load(table[0:1, 0, i:i + 1] if peeled else table[0:1, 0, bass.ds(i, 1)], min_val=0, max_val=E - 1)

            transpose_rows(0, 0, True)
            transpose_rows(1, 1, True)
            hidden(0, 0, True)
            for i in range(SLOTS):
                e = expert_of(i, True)
                if i + 1 < SLOTS:
                    hidden(i + 1, (i + 1) % 3, True)
                if i + 2 < SLOTS:
                    transpose_rows(i + 2, (i + 2) % 3, True)
                expert_out(i, i % 3, e, True)

_INS = ['L0_attn_x', 'L0_attn_Wq', 'L0_attn_Wk', 'L0_attn_Wv', 'L0_attn_Wg', 'L0_attn_Wgk1', 'L0_attn_Wgk2', 'L0_attn_bgk2', 'L0_attn_Wo', 'L0_attn_g_norm_weight', 'L0_ffn_Wr', 'L0_ffn_br', 'L0_ffn_W1', 'L0_ffn_b1', 'L0_ffn_W2', 'L0_ffn_b2']
_OUTS = [((1, 2048, 128), 'float32')]


def kernel(**inputs):
    import numpy as _np
    import concourse.bacc as _bacc
    from concourse import mybir as _mybir
    from concourse.bass_utils import run_bass_kernel_spmd as _run

    nc = _bacc.Bacc("TRN2", target_bir_lowering=False, num_devices=1)
    arrays, args = {}, []
    for name in _INS:
        a = _np.ascontiguousarray(inputs[name])
        arrays[f"in_{name}_dram"] = a
        args.append(nc.dram_tensor(f"in_{name}_dram", a.shape, _mybir.dt.from_np(a.dtype), kind="ExternalInput").ap())
    for i, (shape, dtype) in enumerate(_OUTS):
        dt = _mybir.dt.from_np(_np.dtype(dtype))
        args.append(nc.dram_tensor(f"out_{i}_dram", shape, dt, kind="ExternalOutput").ap())
    build(nc, *args)
    r = _run(nc, [arrays], core_ids=[0])
    got = tuple(r.results[0][f"out_{i}_dram"] for i in range(len(_OUTS)))
    return got[0]
```

```python
from contextlib import ExitStack

import concourse.bass as bass
from concourse import mybir

F32 = mybir.dt.float32
BF16 = mybir.dt.bfloat16
I32 = mybir.dt.int32
U32 = mybir.dt.uint32
ACT = mybir.ActivationFunctionType
ALU = mybir.AluOpType
AX_X = mybir.AxisListType.X

P = 128
HEADS = 4
EPS = 1e-5
GATE_NORMALIZER = 16.0
GROUP = 512
SAFE = 80.0
TOP = 2
FT = 2
AHEAD = 6


def build(nc, x, Wq, Wk, Wv, Wg, Wgk1, Wgk2, bgk2, Wo, g_norm, Wr, br, W1, b1, W2, b2, out):
    _, N, D = x.shape
    R = Wgk1.shape[1]
    DV = Wv.shape[1]
    E = Wr.shape[1]
    H = W1.shape[2]
    dk = P // HEADS
    dv = DV // HEADS
    T = N // P
    NG = N // GROUP
    TG = GROUP // P
    MID = P // 2 - 1
    HC = H // P
    DVC = DV // P
    NB = T // 2
    CAP = N + P
    ROW = D + 2
    SLOTS = (TOP * N - E) // P + E
    assert T <= 256 and T * E == P and D == P and Wq.shape[1] == P and T % 2 == 0


    x_tok = x.rearrange("a (t p) d -> p (a t) d", p=P)
    out_tok = out.rearrange("a (t p) d -> p (a t) d", p=P)
    rows = nc.dram_tensor("expert_rows", [E * CAP, ROW], F32, kind="Internal").ap()
    results = nc.dram_tensor("expert_results", [TOP * N, D], F32, kind="Internal").ap()

    with ExitStack() as ctx:
        def sb(name, shape, dt=F32):
            return ctx.enter_context(nc.sbuf_tensor(name, shape, dt))

        def sem(name):
            return ctx.enter_context(nc.semaphore(name))

        x_sb = sb("x_sb", [P, T, D])
        wq_sb = sb("wq_sb", [P, P])
        wk_sb = sb("wk_sb", [P, P])
        wv_sb = sb("wv_sb", [P, DV])
        wg_sb = sb("wg_sb", [P, DV])
        wgk1_sb = sb("wgk1_sb", [P, R])
        wgk2_sb = sb("wgk2_sb", [R, P])
        bgk2_sb = sb("bgk2_sb", [P, 1])
        wo_in = sb("wo_in", [P, DVC, D])
        gnorm_sb = sb("gnorm_sb", [P, 1])
        wr_sb = sb("wr_sb", [P, E])
        br_sb = sb("br_sb", [P, E])
        b1_in = sb("b1_in", [E * HC, P])
        b1_sb = sb("b1_sb", [P, E * HC])
        w2_sb = sb("w2_sb", [P, E, HC * D])
        b2_sb = sb("b2_sb", [P, E, D])
        ident = sb("ident", [P, P])
        causal = sb("causal", [P, P])
        keep = sb("keep", [P, P], I32)
        before = sb("before", [P, P])
        before_count = sb("before_count", [P, P], BF16)
        ones_count = sb("ones_count", [P, P], BF16)
        head_pick = sb("head_pick", [P, HEADS])
        block_ones = sb("block_ones", [P, P])
        seg = sb("seg", [P, GROUP])
        eps_sb = sb("eps_sb", [P, 1])
        expert_id = sb("expert_id", [P, E])
        expert_row = sb("expert_row", [P, E])
        slot_id = sb("slot_id", [P, SLOTS])
        pad_row = sb("pad_row", [P, ROW])
        xT = sb("xT", [P, N])
        wgk1T = sb("wgk1T", [R, P])
        wgk = sb("wgk", [P, P])
        wo_sb = sb("wo_sb", [P, DVC, D])
        qT = sb("qT", [P, N])
        kT = sb("kT", [P, N])
        gT = sb("gT", [P, N])
        cum = sb("cum", [P, N])
        dist = sb("dist", [P, 2, GROUP])
        eq = sb("eq", [P, 2, GROUP])
        ek = sb("ek", [P, 2, GROUP])
        rest = sb("rest", [P, T])
        em = sb("em", [P, T])
        er = sb("er", [P, T])
        tile_decay = sb("tile_decay", [P, T])
        qm = sb("qm", [P, N])
        km = sb("km", [P, N])
        soft, zb = qm, km
        qc = sb("qc", [P, N])
        kc = sb("kc", [P, N])
        v_sb = sb("v_sb", [P, T, DV])
        gate = sb("gate", [P, DVC, N])
        aT = sb("aT", [P, 2, HEADS, P])
        kcT = sb("kcT", [P, 2, P])
        state = sb("state", [P, 2, DV])
        sq = sb("sq", [P, 2, DVC, P])
        lrms = sb("lrms", [P, DVC, P])
        rrms = sb("rrms", [P, 2, DVC, P])
        rgate = sb("rgate", [P, 2, DVC, P])
        ogT = sb("ogT", [P, 2, DVC, P])
        res = sb("res", [P, 2, D])
        stats = sb("stats", [P, 2, 6])
        mv = sb("mv", [P, 2, 2])
        lstd = sb("lstd", [P, 2, 1])
        rstd = sb("rstd", [P, 2, 1])
        x1T = sb("x1T", [P, 2, P])
        xr = sb("xr", [P, T, TOP, ROW])
        score = sb("score", [P, T, E])
        top8 = sb("top8", [P, T, 8])
        top_at = sb("top_at", [P, T, 8], U32)
        top_f = sb("top_f", [P, T, TOP])
        hot = sb("hot", [P, T, TOP, E])
        hit = sb("hit", [P, T, E], BF16)
        so_far = sb("so_far", [P, T + 1, E], BF16)
        gap = sb("gap", [P, T])
        egap = sb("egap", [P, T])
        log_sum = sb("log_sum", [P, T])
        place = sb("place", [P, T, E])
        placed = sb("placed", [P, T, TOP, E])
        slot_f = sb("slot_f", [P, T, TOP])
        slot = sb("slot", [P, T, TOP], U32)
        pair_id = sb("pair_id", [P, 1])
        pair_pick = sb("pair_pick", [P, E])
        pair_pick_id = sb("pair_pick_id", [P, E])
        pair_n = sb("pair_n", [P, 1])
        pair_first = sb("pair_first", [P, 1])
        pair_next = sb("pair_next", [P, 1])
        pair_value = sb("pair_value", [P, 3])
        pair_counts = sb("pair_counts", [P, NB, E])
        pair_count = sb("pair_count", [P, NB])
        pair_full = sb("pair_full", [P, 1])
        pair_used = sb("pair_used", [P, 1])
        pair_short = sb("pair_short", [P, NB])
        pair_slot = sb("pair_slot", [P, 1])
        in_slot = sb("in_slot", [P, SLOTS])
        table = sb("table", [1, 3, SLOTS], I32)
        xg = sb("xg", [P, AHEAD, ROW])
        w1_buf = [m[:, n * H:(n + 1) * H] for m in (km, qm) for n in range(AHEAD // 2)]
        xgT, yb = (kT[:, 3 * D * n:3 * D * (n + 1)].rearrange("p (u d) -> p u d", d=D) for n in range(2))
        yw = kT[:, 6 * D:(6 + AHEAD) * D].rearrange("p (u d) -> p u d", d=D)
        hT = gT[:, 0:3 * H].rearrange("p (u j t) -> p u j t", j=HC, t=P)
        dest = sb("dest", [P, AHEAD], U32)
        ysum = gate[:, :, :].rearrange("p c n -> p (c n)").rearrange("p (t d) -> p t d", d=TOP * D)
        assert DV == TOP * D
        acc = xT[:, :].rearrange("p (t d) -> p t d", d=D)
        fstats = sb("fstats", [P, T, 6])
        fmv = sb("fmv", [P, T, 2])
        flog = sb("flog", [P, T])
        frstd = sb("frstd", [P, T])
        fshift = sb("fshift", [P, T])
        result = x_sb
        span = sb("span", [P, 2, T])
        widest = sb("widest", [P, 1])
        worst = sb("worst", [1, 1])
        wide_flag = sb("wide_flag", [1, 1], I32)
        decay, outer, states, q_states = qm, km, kc, kc
        v_col = xr[:, :, 0, 0:D].rearrange("p t (h k) -> p t h k", k=dk)
        v_heads = v_sb[:, :, :].rearrange("p t (h v) -> p t h v", v=dv)

        psum = ctx.enter_context(nc.psum_tensor("psum", [P, 8, 512], F32))
        bank = [psum[:, i, :] for i in range(8)]

        s_x = [sem(f"x_loaded{g}") for g in range(NG)]
        s_gatew = sem("gate_weights_loaded")
        s_projw = sem("projection_weights_loaded")
        s_vgw = sem("value_weights_loaded")
        s_wo = sem("wo_loaded")
        s_router = sem("router_loaded")
        s_b1 = sem("b1_loaded")
        s_w2 = sem("w2_loaded")
        s_seed = sem("constants_zeroed")
        s_const = sem("constants_made")
        s_dinit = sem("vector_buffers_set")
        s_job = sem("projection_in_psum")
        s_jact = sem("act_emptied_bank")
        s_jdve = sem("dve_emptied_bank")
        s_wo2 = sem("wo_scaled")
        s_abs = sem("abs_done")
        s_exp = sem("exp_done")
        s_soft = sem("softplus_done")
        s_g = sem("gate_log_done")
        s_cum = sem("cumsum_done")
        s_rest = sem("rest_done")
        s_span = sem("decay_spans_done")
        s_dist0 = sem("distance_done")
        s_dist = sem("distance_clamped")
        s_small = sem("tile_factors_done")
        s_eq = sem("decay_factors_done")
        s_qm = sem("qm_done")
        s_qc = sem("qc_done")
        s_km = sem("km_done")
        s_kc = sem("kc_done")
        s_widest = sem("widest_span_of_channels")
        s_flag = sem("range_flag_ready")
        s_turn = sem("general_path_turn")
        s_a = sem("scores_in_psum")
        s_aT = sem("scores_masked")
        s_act_bank = sem("act_bank_written")
        s_dve_bank = sem("dve_bank_written")
        s_kcT = sem("kc_copied")
        s_state = sem("state_updated")
        s_o = sem("o_in_psum")
        s_sq = sem("o_squared")
        s_lrms = sem("log_rms_done")
        s_rr = sem("rrms_done")
        s_rg = sem("gate_over_rms_done")
        s_og = sem("o_gated")
        s_res = sem("residual_done")
        s_st = sem("stats_done")
        s_mv = sem("mean_var_done")
        s_lstd = sem("log_std_done")
        s_rstd = sem("rstd_done")
        s_x1 = sem("x1_done")
        s_x1T = sem("x1T_copied")
        s_score = sem("score_kept")
        s_top = sem("top8_found")
        s_topat = sem("top_indices_found")
        s_topf = sem("top_indices_as_float")
        s_hot = sem("one_hot_done")
        s_hit = sem("hits_done")
        s_sofar = sem("running_hits_done")
        s_gap = sem("gap_done")
        s_egap = sem("exp_gap_done")
        s_log_sum = sem("log_weight_sum_done")
        s_w1st = sem("first_weight_done")
        s_weight = sem("weights_done")
        s_place0 = sem("places_taken")
        s_placed = sem("places_picked")
        s_slotf = sem("slots_as_float")
        s_slot = sem("slots_done")
        s_xcopy = sem("second_rows_copied")
        s_pad = sem("rows_padded")
        s_scat = [sem(f"rows_scattered{u}") for u in range(2)]
        s_rows = sem("batches_in_dram")
        s_pair = sem("pair_constant")
        s_pos = sem("pair_positions_in_psum")
        s_entries = sem("entries_in_psum")
        s_tab = sem("table_step")
        s_table = sem("table_done")
        s_xg = [sem(f"rows_gathered{u}") for u in range(AHEAD)]
        s_w1 = [sem(f"w1_gathered{u}") for u in range(AHEAD)]
        s_gt = sem("rows_transposed")
        s_gT = sem("rows_transposed_copied")
        s_ha = sem("hidden_lower_in_psum")
        s_hb = sem("hidden_upper_in_psum")
        s_hTa = sem("hidden_lower_done")
        s_hTb = sem("hidden_upper_done")
        s_ye = sem("expert_out_in_psum")
        s_yb = sem("expert_out_biased")
        s_yw = sem("expert_out_weighted")
        s_dest = sem("destinations_done")
        s_out = [sem(f"results_scattered{u}") for u in range(AHEAD)]
        s_ysum = [sem(f"results_loaded{g}") for g in range(T // FT)]
        s_acc0 = sem("first_result_added")
        s_acc = sem("second_result_added")
        s_fst = sem("final_stats")
        s_fmv = sem("final_mean_var")
        s_flog = sem("final_log")
        s_frs = sem("final_rstd")
        s_fshift = sem("final_shift")
        s_result = sem("result_done")
        s_stored = sem("stored")

        jobs = [("xT", 0, "dve"), ("wgk1T", 0, "dve"), ("wgk", 0, "dve")]
        for g in range(1, NG):
            jobs += [("xT", g, "act" if g % 2 else "dve"), ("z", g - 1, "dve")]
        jobs += [("z", NG - 1, "dve")]
        for g in range(NG):
            jobs += [("q", g, "act"), ("k", g, "act"), ("v", 2 * g, "dve"), ("v", 2 * g + 1, "dve")]
        jobs += [("g", g, "act") for g in range(NG)]
        jobs += [("b1T", 0, "dve"), ("span", 0, "dve")]
        jobs += [("g", g, "act") for g in range(NG, 2 * NG)]
        at = {job[:2]: i for i, job in enumerate(jobs)}

        def emptied(i):
            engine = jobs[i][2]
            return (s_jact if engine == "act" else s_jdve), sum(j[2] == engine for j in jobs[:i + 1])

        def bank_of(kind, g):
            return bank[at[kind, g] % 8]

        n_act = sum(j[2] == "act" for j in jobs)
        n_dve = len(jobs) - n_act

        def tiles(ap):
            return ap.rearrange("p (n c) -> p n c", c=P)

        def wide(ap, n):
            return ap.unsqueeze(2).to_broadcast([ap.shape[0], ap.shape[1], n])

        V_STEPS = 5 + 2 * NG
        V_END = 1 + dv * V_STEPS

        AGE_O, AGE_GATE, AGE_OUT, AGE_X1T, AGE_ROUTE, AGE_PLACE = 1, 2, 3, 4, 5, 6
        ROUNDS = T + AGE_PLACE

        def factor_round(g):
            return (TG - 1) * (g - 1)

        groups_begun = {factor_round(g): g for g in range(1, NG)}
        groups_ended = {factor_round(g) + 1: g for g in range(1, NG)}

        def at_age(i, age):
            return i - age if 0 <= i - age < T else None

        def batch_at(i, lag):
            t = i - lag
            return t // 2 if 0 <= t < T and t % 2 else None

        def expert_of(engine, i):
            return engine.value_load(table[0:1, 0, i:i + 1], min_val=0, max_val=E - 1)

        def pool_loads_w1(i):
            return i % 3 == 2

        def gather_w1(engine, i):
            e = expert_of(engine, i)
            if i >= AHEAD:
                engine.wait_ge(s_hb, i - AHEAD + 1)
            engine.dma_start(w1_buf[i % AHEAD], W1[bass.ds(e, 1), :, :].rearrange("a p h -> p (a h)")).then_inc(s_w1[i % AHEAD], 16)

        block = ctx.enter_context(nc.Block())

        @block.sync
        def _(sp):
            for g in range(NG):
                sp.dma_start(x_sb[:, g * TG:(g + 1) * TG, :], x_tok[:, g * TG:(g + 1) * TG, :]).then_inc(s_x[g], 16)
            sp.dma_start(wv_sb[:, :], Wv).then_inc(s_vgw, 16)
            sp.dma_start(wg_sb[:, :], Wg).then_inc(s_vgw, 16)
            sp.dma_start(wo_in[:, :, :], Wo.rearrange("(c p) d -> p c d", p=P)).then_inc(s_wo, 16)
            for c in range(P // dv):
                sp.dma_start(gnorm_sb[c * dv:(c + 1) * dv, :], g_norm.rearrange("(p a) -> p a", a=1)).then_inc(s_wo, 16)
            sp.wait_ge(s_const, 4)
            for e in range(E):
                sp.dma_start(rows[e * CAP:(e + 1) * CAP, :].rearrange("(n p) c -> p n c", p=P),
                             pad_row[:, :].unsqueeze(1).to_broadcast([P, CAP // P, ROW])).then_inc(s_pad, 16)
            sp.dma_start(w2_sb[:, :, :].rearrange("p e (j d) -> p e j d", d=D),
                         W2.rearrange("e (j p) d -> p e j d", p=P)).then_inc(s_w2, 16)
            sp.dma_start(b2_sb[:, :, :], b2.partition_broadcast(P)).then_inc(s_w2, 16)

            sp.wait_ge(s_table, 3)
            def gather(i):
                u = i % AHEAD
                r = sp.value_load(table[0:1, 1, i:i + 1], min_val=0, max_val=E * CAP - P)
                if i < 3:
                    sp.wait_ge(s_rows, sp.value_load(table[0:1, 2, i:i + 1], min_val=1, max_val=NB))
                elif i == 3:
                    sp.wait_ge(s_rows, NB)
                if i >= AHEAD:
                    sp.wait_ge(s_yw, i - AHEAD + 1)
                    sp.wait_ge(s_dest, i - AHEAD + 1)
                sp.dma_start(xg[:, u, :], rows[bass.ds(r, P), :]).then_inc(s_xg[u], 16)
                if not pool_loads_w1(i):
                    gather_w1(sp, i)

            for i in range(SLOTS):
                gather(i)
            for u in range(AHEAD):
                sp.wait_ge(s_out[u], 16 * len(range(u, SLOTS, AHEAD)))
            for g in range(T // FT):
                sp.dma_start(ysum[:, g * FT:(g + 1) * FT, :],
                             results[g * FT * P * TOP:(g + 1) * FT * P * TOP, :].rearrange("(t p k) d -> p t (k d)", p=P, k=TOP)).then_inc(s_ysum[g], 16)
            for g in range(T // FT):
                sp.wait_ge(s_result, (g + 1) * FT)
                sp.dma_start(out_tok[:, g * FT:(g + 1) * FT, :], result[:, g * FT:(g + 1) * FT, :]).then_inc(s_stored, 16)
            sp.wait_ge(s_stored, 16 * (T // FT))

        @block.gpsimd
        def _(pool):
            pool.memset(ident[:, :], 0.0).then_inc(s_seed, 1)
            pool.memset(causal[:, :], 1.0).then_inc(s_seed, 1)
            pool.memset(before[:, :], 1.0).then_inc(s_seed, 1)
            pool.memset(head_pick[:, :], 0.0).then_inc(s_seed, 1)
            pool.memset(block_ones[:, :], 0.0).then_inc(s_seed, 1)
            pool.memset(pad_row[:, :], 0.0).then_inc(s_seed, 1)
            n = [0]

            def const(ins):
                n[0] += 1
                ins.then_inc(s_const, 1)
                pool.wait_ge(s_const, n[0])

            pool.wait_ge(s_seed, 6)
            const(pool.affine_select(out=ident[:, :], in_=ident[:, :], compare_op=ALU.not_equal, fill=1.0,
                                     base=0, pattern=[[-1, P]], channel_multiplier=1))
            const(pool.affine_select(out=causal[:, :], in_=causal[:, :], compare_op=ALU.is_ge, fill=0.0,
                                     base=0, pattern=[[1, P]], channel_multiplier=-1))
            const(pool.affine_select(out=before[:, :], in_=before[:, :], compare_op=ALU.is_ge, fill=0.0,
                                     base=-1, pattern=[[1, P]], channel_multiplier=-1))
            def count_up(ap, pattern, base, channel):
                const(pool.iota(ap, pattern=pattern, base=base, channel_multiplier=channel,
                                allow_small_or_imprecise_dtypes=True))

            count_up(pad_row[:, ROW - 1:ROW], [[1, 1]], TOP * N, 1)
            for h in range(HEADS):
                const(pool.memset(head_pick[h * dk:(h + 1) * dk, h:h + 1], 1.0))
            for c in range(P // dv):
                const(pool.memset(block_ones[c * dv:(c + 1) * dv, c * dv:(c + 1) * dv], 1.0))

            count_up(expert_id[:, :], [[1, E]], 0, 0)
            count_up(expert_row[:, :], [[CAP, E]], 0, 0)
            count_up(pair_id[:, :], [[1, 1]], 0, 1)
            count_up(slot_id[:, :], [[1, SLOTS]], 0, 0)
            count_up(xr[:, :, :, ROW - 1], [[TOP * P, T], [1, TOP]], 0, TOP)
            def scale_k(g):
                c = slice(g * GROUP, (g + 1) * GROUP)
                t = slice(g * TG, (g + 1) * TG)
                pool.wait_ge(s_eq, 2 * (g + 1))
                pool.tensor_tensor(km[:, c], kT[:, c], ek[:, g % 2, :], ALU.mult).then_inc(s_km, 1)
                pool.wait_ge(s_km, g + 1)
                pool.tensor_tensor(tiles(kc[:, c]), tiles(km[:, c]), wide(er[:, t], P), ALU.mult).then_inc(s_kc, 1)

            scale_k(0)

            def gate_over_rms(t):
                pool.wait_ge(s_rr, t + 1)
                if t >= 2:
                    pool.wait_ge(s_og, t - 1)
                pool.tensor_tensor(rgate[:, t % 2, :, :], rrms[:, t % 2, :, :], gate[:, :, t * P:(t + 1) * P],
                                   ALU.mult).then_inc(s_rg, 1)

            def tell_batch(b):
                pool.wait_ge(s_scat[b % 2], 32 * TOP * (b // 2 + 1))
                pool.sem_inc(s_rows, 1)

            def scatter_rows(t):
                for k in range(TOP):
                    pool.indirect_dma_start(out=rows[:, :], in_=xr[:, t, k, :], in_offset=None,
                                            out_offset=bass.IndirectOffsetOnAxis(ap=slot[:, t, k:k + 1], axis=0)
                                            ).then_inc(s_scat[t // 2 % 2], 16)

            pool.wait_ge(s_pad, 16 * E)
            pool.wait_ge(s_jact, n_act)
            for i in range(ROUNDS + 2):
                t = at_age(i, AGE_GATE)
                if t is not None:
                    gate_over_rms(t)
                if i in groups_ended:
                    scale_k(groups_ended[i])
                b = batch_at(i, AGE_PLACE + 1)
                if b is not None:
                    tt = slice(2 * b, 2 * b + 2)
                    pool.wait_ge(s_w1st, b + 1)
                    pool.tensor_tensor(xr[:, tt, 1, D], egap[:, tt], xr[:, tt, 0, D], ALU.mult).then_inc(s_weight, 1)
                    pool.wait_ge(s_slot, b + 1)
                    pool.wait_ge(s_weight, b + 1)
                    pool.wait_ge(s_xcopy, 2 * (b + 1))
                    if b >= 2:
                        tell_batch(b - 2)
                    scatter_rows(2 * b)
                b = batch_at(i, AGE_PLACE + 2)
                if b is not None:
                    scatter_rows(2 * b + 1)
            tell_batch(NB - 2)
            tell_batch(NB - 1)
            pool.wait_ge(s_table, 3)

            for i in range(AHEAD - 1):
                if pool_loads_w1(i):
                    gather_w1(pool, i)

            def scatter_results(i):
                u = i % AHEAD
                pool.wait_ge(s_xg[u], (i // AHEAD + 1) * 16)
                if i >= AHEAD:
                    pool.wait_ge(s_out[u], (i // AHEAD) * 16)
                pool.tensor_copy(dest[:, u:u + 1], xg[:, u, ROW - 1:ROW]).then_inc(s_dest, 1)
                pool.wait_ge(s_dest, i + 1)
                pool.wait_ge(s_yw, i + 1)
                pool.indirect_dma_start(out=results[:, :], in_=yw[:, u, :], in_offset=None,
                                        bounds_check=TOP * N - 1, oob_is_err=False,
                                        out_offset=bass.IndirectOffsetOnAxis(ap=dest[:, u:u + 1], axis=0)
                                        ).then_inc(s_out[u], 16)

            for i in range(SLOTS):
                scatter_results(i)
                if i + AHEAD - 1 < SLOTS and pool_loads_w1(i + AHEAD - 1):
                    gather_w1(pool, i + AHEAD - 1)
            for g in range(T // FT):
                t = slice(g * FT, (g + 1) * FT)
                pool.wait_ge(s_ysum[g], 16)
                pool.tensor_tensor(acc[:, t, :], ysum[:, t, 0:D], xr[:, t, 0, 0:D], ALU.add).then_inc(s_acc0, 1)

        @block.scalar
        def _(act):
            act.dma_start(wgk1_sb[:, :], Wgk1).then_inc(s_gatew, 16)
            act.dma_start(wgk2_sb[:, :], Wgk2).then_inc(s_gatew, 16)
            act.dma_start(bgk2_sb[:, :], bgk2.rearrange("(p a) -> p a", a=1)).then_inc(s_gatew, 16)
            act.dma_start(wq_sb[:, :], Wq).then_inc(s_projw, 16)
            act.dma_start(wk_sb[:, :], Wk).then_inc(s_projw, 16)
            act.dma_start(wr_sb[:, :], Wr).then_inc(s_router, 16)
            act.dma_start(br_sb[:, :], br.partition_broadcast(P)).then_inc(s_router, 16)
            act.dma_start(b1_in[:, :], b1.rearrange("e (j p) -> (e j) p", p=P)).then_inc(s_b1, 16)
            act.preload_act_table_set("natural_log_exp_and_others")

            def softplus(g):
                c = slice(g * GROUP, (g + 1) * GROUP)
                act.wait_ge(s_jdve, emptied(at["z", g])[1])
                act.activation(soft[:, c], zb[:, c], ACT.Abs).then_inc(s_abs, 1)
                act.wait_ge(s_abs, g + 1)
                act.activation(soft[:, c], soft[:, c], ACT.Exp, scale=-1.0).then_inc(s_exp, 1)
                act.wait_ge(s_exp, g + 1)
                act.activation(soft[:, c], soft[:, c], ACT.Ln, bias=1.0).then_inc(s_soft, 1)

            def take_qk(g):
                c = slice(g * GROUP, (g + 1) * GROUP)
                act.wait_ge(s_job, at["q", g] + 1)
                act.activation(qT[:, c], bank_of("q", g)[:, :], ACT.Copy, scale=float(dk) ** -0.5).then_inc(s_jact, 1)
                act.wait_ge(s_job, at["k", g] + 1)
                act.activation(kT[:, c], bank_of("k", g)[:, :], ACT.Copy).then_inc(s_jact, 1)

            def factors(g):
                if g == 0:
                    act.wait_ge(s_cum, NG)
                    act.wait_ge(s_rest, NG)
                    ct = tiles(cum[:, :])
                    act.activation(em[:, :], ct[:, :, MID], ACT.Exp, scale=1 / GATE_NORMALIZER).then_inc(s_small, 1)
                    act.activation(er[:, :], rest[:, :], ACT.Exp, scale=1 / GATE_NORMALIZER).then_inc(s_small, 1)
                    act.activation(tile_decay[:, :], ct[:, :, P - 1], ACT.Exp, scale=1 / GATE_NORMALIZER).then_inc(s_small, 1)
                act.wait_ge(s_dist, g + 1)
                if g >= 2:
                    act.wait_ge(s_qm, g - 1)
                    act.wait_ge(s_km, g - 1)
                act.activation(eq[:, g % 2, :], dist[:, g % 2, :], ACT.Exp, scale=1 / GATE_NORMALIZER).then_inc(s_eq, 1)
                act.activation(ek[:, g % 2, :], dist[:, g % 2, :], ACT.Exp, scale=-1 / GATE_NORMALIZER).then_inc(s_eq, 1)

            act.wait_ge(s_dinit, 9)
            for g in range(1, NG, 2):
                act.wait_ge(s_job, at["xT", g] + 1)
                act.activation(xT[:, g * GROUP:(g + 1) * GROUP], bank_of("xT", g), ACT.Copy).then_inc(s_jact, 1)
            for g in range(NG):
                softplus(g)
                take_qk(g)
            factors(0)
            for g in range(2 * NG):
                act.wait_ge(s_job, at["g", g] + 1)
                act.activation(gate[:, g % DVC, g // DVC * GROUP:(g // DVC + 1) * GROUP], bank_of("g", g),
                               ACT.Silu).then_inc(s_jact, 1)

            act.wait_ge(s_flag, 1)
            too_wide = act.value_load(wide_flag[0:1, 0:1], min_val=0, max_val=1)
            with act.If(too_wide):
                act.wait_ge(s_qc, 1)
                act.wait_ge(s_kc, 1)
                act.preload_act_table_set("natural_log_exp_and_others")
                act.activation(decay[:, :], gT[:, :], ACT.Exp, scale=1 / GATE_NORMALIZER).then_inc(s_turn, 1)

            act.preload_act_table_set("natural_log_exp_and_others")

            def inverse_rms(t):
                act.activation(lrms[:, :, :], bank[6][:, 256:512].rearrange("p (c t) -> p c t", t=P), ACT.Ln,
                               bias=eps_sb[:, :], scale=1.0 / dv).then_inc(s_lrms, 1)
                act.wait_ge(s_lrms, t + 1)
                if t >= 2:
                    act.wait_ge(s_rg, t - 1)
                act.activation(rrms[:, t % 2, :, :], lrms[:, :, :], ACT.Exp, scale=-0.5).then_inc(s_rr, 1)

            def copy_kcT(t):
                act.activation(kcT[:, t % 2, :], bank[6][:, 0:P], ACT.Copy).then_inc(s_kcT, 1)

            def copy_x1T(t):
                if t >= 2:
                    act.wait_ge(s_dve_bank, t - 2 + AGE_ROUTE)
                act.activation(x1T[:, t % 2, :], bank[6][:, P:2 * P], ACT.Copy).then_inc(s_x1T, 1)

            def copy_row(t):
                act.wait_ge(s_x1, t + 1)
                act.activation(xr[:, t, 1, 0:D], xr[:, t, 0, 0:D], ACT.Copy).then_inc(s_xcopy, 1)

            def inverse_std(t):
                b = t % 2
                act.wait_ge(s_mv, t + 1)
                act.activation(lstd[:, b, :], mv[:, b, 1:2], ACT.Ln, bias=eps_sb[:, :]).then_inc(s_lstd, 1)
                act.wait_ge(s_lstd, t + 1)
                if t >= 2:
                    act.wait_ge(s_x1, t - 1)
                act.activation(rstd[:, b, :], lstd[:, b, :], ACT.Exp, scale=-0.5).then_inc(s_rstd, 1)

            def square_o(t):
                act.wait_ge(s_o, t + 1)
                act.activation(sq[:, t % 2, :, :], bank[4 + t % 2][:, 0:DV].rearrange("p (c t) -> p c t", t=P),
                               ACT.Square).then_inc(s_sq, 1)

            def exp_gap(b):
                act.wait_ge(s_gap, b + 1)
                tt = slice(2 * b, 2 * b + 2)
                act.activation(egap[:, tt], gap[:, tt], ACT.Exp).then_inc(s_egap, 1)
                act.wait_ge(s_egap, b + 1)
                act.activation(log_sum[:, tt], egap[:, tt], ACT.Ln, bias=1.0).then_inc(s_log_sum, 1)
                act.wait_ge(s_log_sum, b + 1)
                act.activation(xr[:, tt, 0, D], log_sum[:, tt], ACT.Exp, scale=-1.0).then_inc(s_w1st, 1)

            for i in range(ROUNDS):
                if i <= T - 1 + AGE_X1T:
                    act.wait_ge(s_act_bank, i + 1)
                for age, stage in ((AGE_GATE, inverse_rms), (0, copy_kcT), (AGE_X1T, copy_x1T), (AGE_X1T, copy_row)):
                    t = at_age(i, age)
                    if t is not None:
                        stage(t)
                b = batch_at(i, AGE_PLACE)
                if b is not None:
                    exp_gap(b)
                for age, stage in ((AGE_OUT, inverse_std), (AGE_O, square_o)):
                    t = at_age(i, age)
                    if t is not None:
                        stage(t)
                if i in groups_begun:
                    factors(groups_begun[i])

            act.wait_ge(s_table, 3)

            def copy_rows(i):
                h = i % 3
                act.wait_ge(s_gt, i + 1)
                if i >= 3:
                    act.wait_ge(s_hb, i - 2)
                act.activation(xgT[:, h, :], bank[7][:, 0:P], ACT.Copy).then_inc(s_gT, 1)

            def hidden_lower(i):
                h = i % 3
                e = expert_of(act, i)
                act.wait_ge(s_ha, i + 1)
                if i >= 3:
                    act.wait_ge(s_ye, i - 2)
                for n in range(HC // 2):
                    act.activation(hT[:, h, n, :], bank[2 * (i % 2)][:, n * P:(n + 1) * P], ACT.Relu,
                                   bias=b1_sb[:, bass.ds(e * HC + n, 1)]).then_inc(s_hTa, 1)

            def act_step(i):
                hidden_lower(i)
                if i + 2 < SLOTS:
                    copy_rows(i + 2)

            copy_rows(0)
            copy_rows(1)
            for i in range(SLOTS):
                act_step(i)
            for g in range(T // FT + 1):
                if g < T // FT:
                    t = slice(g * FT, (g + 1) * FT)
                    act.wait_ge(s_fmv, (g + 1) * FT)
                    act.activation(flog[:, t], fmv[:, t, 1], ACT.Ln, bias=eps_sb[:, :]).then_inc(s_flog, 1)
                    act.wait_ge(s_flog, g + 1)
                    act.activation(frstd[:, t], flog[:, t], ACT.Exp, scale=-0.5).then_inc(s_frs, 1)
                if g:
                    act.wait_ge(s_frs, g)
                    act.wait_ge(s_fshift, g)
                    for n in range((g - 1) * FT, g * FT):
                        act.activation(result[:, n, :], acc[:, n, :], ACT.Identity, bias=fshift[:, n:n + 1],
                                       scale=frstd[:, n:n + 1]).then_inc(s_result, 1)

        @block.vector
        def _(dve):
            dve.memset(seg[:, :], 1.0).then_inc(s_dinit, 1)
            dve.memset(ones_count[:, :], 1.0).then_inc(s_dinit, 1)
            dve.memset(aT[:, :, :, :], 0.0).then_inc(s_dinit, 1)
            dve.memset(eps_sb[:, :], EPS).then_inc(s_dinit, 1)
            dve.memset(so_far[:, 0, :], 0.0).then_inc(s_dinit, 1)
            dve.memset(state[:, :, :], 0.0).then_inc(s_dinit, 1)
            dve.wait_ge(s_dinit, 6)
            dve.memset(seg[:, 0::P], 0.0).then_inc(s_dinit, 1)
            dve.wait_ge(s_const, 3)
            dve.tensor_copy(before_count[:, :], before[:, :]).then_inc(s_dinit, 1)
            dve.tensor_copy(keep[:, :], causal[:, :]).then_inc(s_dinit, 1)

            def take_xT(g):
                dve.wait_ge(s_job, at["xT", g] + 1)
                dve.tensor_copy(xT[:, g * GROUP:(g + 1) * GROUP], bank_of("xT", g)).then_inc(s_jdve, 1)

            def take_z(g):
                dve.wait_ge(s_job, at["z", g] + 1)
                if g == 0:
                    dve.wait_ge(s_gatew, 48)
                dve.tensor_scalar(zb[:, g * GROUP:(g + 1) * GROUP], bank_of("z", g), bgk2_sb[:, 0:1], None,
                                  ALU.add).then_inc(s_jdve, 1)

            take_xT(0)
            dve.wait_ge(s_job, at["wgk1T", 0] + 1)
            dve.tensor_copy(wgk1T[:, :], bank_of("wgk1T", 0)[0:R, 0:P]).then_inc(s_jdve, 1)
            dve.wait_ge(s_job, at["wgk", 0] + 1)
            dve.tensor_copy(wgk[:, :], bank_of("wgk", 0)[:, 0:P]).then_inc(s_jdve, 1)
            for g in range(1, NG):
                if g % 2 == 0:
                    take_xT(g)
                take_z(g - 1)
            take_z(NG - 1)

            def take_v(g):
                dve.wait_ge(s_job, at["v", g] + 1)
                dve.tensor_copy(v_sb[:, 2 * g:2 * g + 2, :], bank_of("v", g).rearrange("p (t v) -> p t v", v=DV)).then_inc(s_jdve, 1)

            def log_decays(g):
                c = slice(g * GROUP, (g + 1) * GROUP)
                t = slice(g * TG, (g + 1) * TG)
                cg = tiles(cum[:, c])
                dve.wait_ge(s_soft, g + 1)
                dve.wait_ge(s_jdve, emptied(at["z", g])[1])
                dve.scalar_tensor_tensor(gT[:, c], zb[:, c], 0.0, soft[:, c], ALU.min, ALU.subtract).then_inc(s_g, 1)
                dve.wait_ge(s_g, g + 1)
                if g == 0:
                    dve.wait_ge(s_dinit, 9)
                dve.tensor_tensor_scan(cum[:, c], seg[:, :], gT[:, c], 0.0, ALU.mult, ALU.add).then_inc(s_cum, 1)
                dve.wait_ge(s_cum, g + 1)
                dve.tensor_tensor(rest[:, t], cg[:, :, P - 1], cg[:, :, MID], ALU.subtract).then_inc(s_rest, 1)
                dve.tensor_tensor(span[:, 0, t], cg[:, :, 0], cg[:, :, MID], ALU.subtract).then_inc(s_span, 1)
                dve.tensor_tensor(span[:, 1, t], cg[:, :, MID], cg[:, :, P - 1], ALU.subtract).then_inc(s_span, 1)

            def distances(g):
                cg = tiles(cum[:, g * GROUP:(g + 1) * GROUP])
                if g >= 2:
                    dve.wait_ge(s_eq, 2 * (g - 1))
                dve.tensor_tensor(tiles(dist[:, g % 2, :]), cg, wide(cg[:, :, MID], P), ALU.subtract).then_inc(s_dist0, 1)
                dve.wait_ge(s_dist0, g + 1)
                dve.tensor_scalar(dist[:, g % 2, :], dist[:, g % 2, :], SAFE * GATE_NORMALIZER, -SAFE * GATE_NORMALIZER,
                                  ALU.min, ALU.max).then_inc(s_dist, 1)

            def scale_q(g):
                c = slice(g * GROUP, (g + 1) * GROUP)
                t = slice(g * TG, (g + 1) * TG)
                dve.wait_ge(s_eq, 2 * g + 1)
                if g == 0:
                    dve.wait_ge(s_jact, emptied(at["k", NG - 1])[1])
                dve.tensor_tensor(qm[:, c], qT[:, c], eq[:, g % 2, :], ALU.mult).then_inc(s_qm, 1)
                dve.wait_ge(s_qm, g + 1)
                dve.tensor_tensor(tiles(qc[:, c]), tiles(qm[:, c]), wide(em[:, t], P), ALU.mult).then_inc(s_qc, 1)

            for g in range(NG):
                log_decays(g)
                if g == 0:
                    distances(0)
                take_v(2 * g)
                take_v(2 * g + 1)
            scale_q(0)
            dve.wait_ge(s_span, 2 * NG)
            dve.tensor_reduce(widest[:, :], span[:, :, :].rearrange("p a n -> p (a n)"), AX_X, ALU.max).then_inc(s_widest, 1)
            dve.wait_ge(s_job, at["b1T", 0] + 1)
            dve.tensor_copy(b1_sb[:, :], bank_of("b1T", 0)[:, 0:E * HC]).then_inc(s_jdve, 1)
            dve.wait_ge(s_job, at["span", 0] + 1)
            dve.tensor_reduce(worst[:, :], bank_of("span", 0)[0:1, 0:P], AX_X, ALU.max).then_inc(s_jdve, 1)
            dve.wait_ge(s_jdve, n_dve)
            dve.tensor_scalar(wide_flag[:, :], worst[:, :], SAFE * GATE_NORMALIZER, None, ALU.is_gt).then_inc(s_flag, 1)

            dve.wait_ge(s_wo, 16 * (1 + P // dv))
            dve.tensor_scalar(wo_sb[:, :, :], wo_in[:, :, :], gnorm_sb[:, 0:1], None, ALU.mult).then_inc(s_wo2, 1)

            pair_step = [0]

            def pair_const(ins):
                pair_step[0] += 1
                ins.then_inc(s_pair, 1)
                dve.wait_ge(s_pair, pair_step[0])

            dve.wait_ge(s_const, 15)
            pair_const(dve.tensor_reduce(pair_pick[:, :], ident[:, :].rearrange("p (n e) -> p e n", e=E), AX_X, ALU.add))
            pair_const(dve.tensor_tensor(pair_pick_id[:, :], pair_pick[:, :], expert_id[:, :], ALU.mult))
            pair_const(dve.tensor_reduce(pair_value[:, 0:1], pair_pick_id[:, :], AX_X, ALU.add))
            pair_const(dve.tensor_tensor(pair_n[:, :], pair_id[:, :], pair_value[:, 0:1], ALU.subtract))
            pair_const(dve.tensor_scalar(pair_first[:, :], pair_n[:, :], float(P // E), None, ALU.mult))
            pair_const(dve.tensor_scalar(pair_next[:, :], pair_first[:, :], float(P), None, ALU.add))
            pair_const(dve.tensor_scalar(pair_value[:, 1:2], pair_value[:, 0:1], float(CAP), float(P - CAP), ALU.mult, ALU.add))
            pair_const(dve.tensor_tensor(pair_value[:, 1:2], pair_value[:, 1:2], pair_first[:, :], ALU.add))

            dve.wait_ge(s_flag, 1)
            too_wide = dve.value_load(wide_flag[0:1, 0:1], min_val=0, max_val=1)
            with dve.If(too_wide):
                with dve.Fori(0, dv) as v:
                    turn = v * V_STEPS + 1
                    dve.wait_ge(s_turn, turn)
                    dve.tensor_scalar(v_col, v_heads[:, :, :, bass.ds(v, 1)].to_broadcast([P, T, HEADS, dk]),
                                      1.0, None, ALU.mult).then_inc(s_turn, 1)
                    for g in range(NG):
                        c = slice(g * GROUP, (g + 1) * GROUP)
                        dve.wait_ge(s_turn, turn + 2 + g)
                        dve.tensor_tensor(outer[:, c], kT[:, c], bank[g], ALU.mult).then_inc(s_turn, 1)
                    dve.wait_ge(s_turn, turn + 2 + NG)
                    dve.tensor_tensor_scan(states[:, :], decay[:, :], outer[:, :], 0.0, ALU.mult, ALU.add).then_inc(s_turn, 1)
                    for g in range(NG):
                        c = slice(g * GROUP, (g + 1) * GROUP)
                        dve.wait_ge(s_turn, turn + 3 + NG + g)
                        dve.tensor_tensor(q_states[:, c], qT[:, c], states[:, c], ALU.mult).then_inc(s_turn, 1)
                    dve.wait_ge(s_turn, turn + 4 + 2 * NG)
                    dve.tensor_scalar(v_heads[:, :, :, bass.ds(v, 1)].rearrange("p t h a -> p t (h a)"),
                                      bank[4][:, 0:T * HEADS].rearrange("p (t h) -> p t h", h=HEADS),
                                      1.0, None, ALU.mult).then_inc(s_turn, 1)
                dve.wait_ge(s_turn, V_END)
                dve.memset(qT[:, :], 1.0 / dk).then_inc(s_turn, 1)
                dve.memset(kT[:, :], 1.0).then_inc(s_turn, 1)
                dve.memset(cum[:, :], 0.0).then_inc(s_turn, 1)
                dve.memset(er[:, :], 0.0).then_inc(s_turn, 1)
                dve.memset(qm[:, 0:GROUP], 1.0 / dk).then_inc(s_turn, 1)
                dve.memset(km[:, 0:GROUP], 1.0).then_inc(s_turn, 1)
                dve.memset(kc[:, 0:GROUP], 0.0).then_inc(s_turn, 1)
                dve.tensor_copy(keep[:, :], ident[:, :]).then_inc(s_turn, 1)
                dve.wait_ge(s_turn, V_END + 8)

            def mask_scores(t):
                dve.wait_ge(s_a, t + 1)
                if t >= 2:
                    dve.wait_ge(s_o, t - 1)
                dve.copy_predicated(aT[:, t % 2, :, :], keep[:, :].unsqueeze(1).to_broadcast([P, HEADS, P]),
                                    psum[:, 0:HEADS, 0:P]).then_inc(s_aT, 1)

            def residual(t):
                dve.tensor_tensor(res[:, t % 2, :], bank[7][:, 256:256 + D], x_sb[:, t, :], ALU.add).then_inc(s_res, 1)

            def update_state(t):
                if t >= 2:
                    dve.wait_ge(s_o, t)
                if t:
                    dve.wait_ge(s_state, HEADS * t)
                for h in range(HEADS):
                    r = slice(h * dk, (h + 1) * dk)
                    v = slice(h * dv, (h + 1) * dv)
                    if t == 0:
                        ins = dve.tensor_copy(state[r, 0, v], bank[7][r, v])
                    else:
                        ins = dve.scalar_tensor_tensor(state[r, t % 2, v], state[r, (t - 1) % 2, v], tile_decay[r, t:t + 1],
                                                       bank[7][r, v], ALU.mult, ALU.add)
                    ins.then_inc(s_state, 1)

            def take_score(t):
                dve.tensor_tensor(score[:, t, :], bank[7][:, 384:384 + E], br_sb[:, :], ALU.add).then_inc(s_score, 1)

            def take_stats(t):
                dve.wait_ge(s_res, t + 1)
                dve.bn_stats(stats[:, t % 2, :], res[:, t % 2, :]).then_inc(s_st, 1)

            def mean_var(t):
                dve.wait_ge(s_st, t + 1)
                if t >= 2:
                    dve.wait_ge(s_x1, t - 1)
                dve.bn_aggr(mv[:, t % 2, :], stats[:, t % 2, :]).then_inc(s_mv, 1)

            def gate_o(t):
                dve.wait_ge(s_rg, t + 1)
                dve.tensor_tensor(ogT[:, t % 2, :, :], bank[4 + t % 2][:, 0:DV].rearrange("p (c t) -> p c t", t=P),
                                  rgate[:, t % 2, :, :], ALU.mult).then_inc(s_og, 1)

            def normalize(t):
                b = t % 2
                dve.wait_ge(s_rstd, t + 1)
                dve.tensor_scalar(xr[:, t, 0, 0:D], res[:, b, :], mv[:, b, 0:1], rstd[:, b, :],
                                  ALU.subtract, ALU.mult).then_inc(s_x1, 1)

            def find_max(b):
                dve.wait_ge(s_score, 2 * b + 2)
                for t in (2 * b, 2 * b + 1):
                    dve.max(top8[:, t, :], score[:, t, :]).then_inc(s_top, 1)

            def find_index(b):
                tt = slice(2 * b, 2 * b + 2)
                dve.wait_ge(s_top, 2 * b + 2)
                for t in (2 * b, 2 * b + 1):
                    dve.max_index(top_at[:, t, :], top8[:, t, :], score[:, t, :]).then_inc(s_topat, 1)
                dve.tensor_tensor(gap[:, tt], top8[:, tt, 1], top8[:, tt, 0], ALU.subtract).then_inc(s_gap, 1)

            def index_to_float(b):
                tt = slice(2 * b, 2 * b + 2)
                dve.wait_ge(s_topat, 2 * b + 2)
                dve.tensor_copy(top_f[:, tt, :], top_at[:, tt, 0:TOP]).then_inc(s_topf, 1)

            def one_hot(b):
                tt = slice(2 * b, 2 * b + 2)
                dve.wait_ge(s_topf, b + 1)
                dve.tensor_tensor(hot[:, tt, :, :], expert_id[:, :].unsqueeze(1).unsqueeze(1).to_broadcast([P, 2, TOP, E]),
                                  top_f[:, tt, :].unsqueeze(3).to_broadcast([P, 2, TOP, E]), ALU.is_equal).then_inc(s_hot, 1)

            def add_hits(b):
                tt = slice(2 * b, 2 * b + 2)
                dve.wait_ge(s_hot, b + 1)
                dve.tensor_tensor(hit[:, tt, :], hot[:, tt, 0, :], hot[:, tt, 1, :], ALU.add).then_inc(s_hit, 1)

            def count_hits(b):
                dve.wait_ge(s_hit, b + 1)
                for t in (2 * b, 2 * b + 1):
                    if t:
                        dve.wait_ge(s_sofar, t)
                    dve.tensor_tensor(so_far[:, t + 1, :], so_far[:, t, :], hit[:, t, :], ALU.add).then_inc(s_sofar, 1)

            def take_places(b):
                tt = slice(2 * b, 2 * b + 2)
                dve.tensor_tensor(place[:, tt, :], bank[7][:, 400:400 + 2 * E].rearrange("p (t e) -> p t e", e=E),
                                  expert_row[:, :].unsqueeze(1).to_broadcast([P, 2, E]), ALU.add).then_inc(s_place0, 1)

            def pick_places(b):
                tt = slice(2 * b, 2 * b + 2)
                dve.wait_ge(s_place0, b + 1)
                dve.tensor_tensor(placed[:, tt, :, :], hot[:, tt, :, :], place[:, tt, :].unsqueeze(2).to_broadcast([P, 2, TOP, E]),
                                  ALU.mult).then_inc(s_placed, 1)

            def sum_places(b):
                tt = slice(2 * b, 2 * b + 2)
                dve.wait_ge(s_placed, b + 1)
                dve.tensor_reduce(slot_f[:, tt, :], placed[:, tt, :, :], AX_X, ALU.add).then_inc(s_slotf, 1)

            def slots_to_int(b):
                tt = slice(2 * b, 2 * b + 2)
                dve.wait_ge(s_slotf, b + 1)
                dve.tensor_copy(slot[:, tt, :], slot_f[:, tt, :]).then_inc(s_slot, 1)

            dve.wait_ge(s_router, 32)
            dve.wait_ge(s_const, 15)
            for i in range(ROUNDS + 1):
                scored = batch_at(i, AGE_ROUTE)
                placing = batch_at(i, AGE_PLACE)
                was_placed = batch_at(i, AGE_PLACE + 1)

                def take(stage, age):
                    t = at_age(i, age)
                    if t is not None:
                        stage(t)

                def take_batch(stage, b):
                    if b is not None:
                        stage(b)

                take_batch(one_hot, placing)
                take_batch(pick_places, was_placed)
                take(mask_scores, 0)
                take_batch(add_hits, placing)
                take_batch(sum_places, was_placed)
                take_batch(count_hits, placing)
                if i >= T:
                    take_batch(slots_to_int, was_placed)
                if 0 < i < ROUNDS:
                    dve.wait_ge(s_dve_bank, i)
                take(residual, AGE_OUT)
                if i < T:
                    take_batch(slots_to_int, was_placed)
                take(take_stats, AGE_OUT)
                take(take_score, AGE_ROUTE)
                take_batch(take_places, placing)
                take(mean_var, AGE_OUT)
                take(update_state, AGE_O)
                take_batch(find_max, scored)
                take(gate_o, AGE_GATE)
                take_batch(find_index, scored)
                take(normalize, AGE_OUT)
                take_batch(index_to_float, scored)
                if i in groups_begun:
                    distances(groups_begun[i])
                if i in groups_ended:
                    scale_q(groups_ended[i])

            step = [0]

            def chain(ins):
                step[0] += 1
                ins.then_inc(s_tab, 1)
                dve.wait_ge(s_tab, step[0])

            chain(dve.tensor_tensor(pair_counts[:, :, :], bank[7][:, 432:432 + NB * E].rearrange("p (b e) -> p b e", e=E),
                                    pair_pick[:, :].unsqueeze(1).to_broadcast([P, NB, E]), ALU.mult))
            chain(dve.tensor_reduce(pair_count[:, :], pair_counts[:, :, :], AX_X, ALU.add))
            chain(dve.tensor_tensor(pair_used[:, :], pair_count[:, NB - 1:NB], pair_first[:, :], ALU.is_gt))
            chain(dve.tensor_tensor(pair_full[:, :], pair_count[:, NB - 1:NB], pair_next[:, :], ALU.min))
            chain(dve.tensor_scalar(pair_short[:, :], pair_count[:, :], pair_full[:, 0:1], None, ALU.is_lt))
            chain(dve.tensor_reduce(pair_value[:, 2:3], pair_short[:, :], AX_X, ALU.add))
            dve.wait_ge(s_pos, 1)
            chain(dve.tensor_copy(pair_slot[:, :], bank[6][:, 0:1]))
            chain(dve.tensor_scalar(in_slot[:, :], slot_id[:, :], pair_slot[:, 0:1], pair_used[:, 0:1], ALU.is_equal, ALU.mult))
            dve.wait_ge(s_entries, 1)
            for k, base in enumerate((0, CAP - P, 1)):
                dve.tensor_scalar(table[:, k, :], bank[6][0:1, 64 * (k + 1):64 * (k + 1) + SLOTS], float(base), None,
                                  ALU.add).then_inc(s_table, 1)
            dve.wait_ge(s_table, 3)

            def hidden_upper(i):
                h = i % 3
                e = expert_of(dve, i)
                dve.wait_ge(s_hb, i + 1)
                if i >= 3:
                    dve.wait_ge(s_ye, i - 2)
                for n in range(HC // 2):
                    dve.tensor_scalar(hT[:, h, HC // 2 + n, :], bank[2 * (i % 2) + 1][:, n * P:(n + 1) * P],
                                      b1_sb[:, bass.ds(e * HC + HC // 2 + n, 1)], 0.0, ALU.add, ALU.max).then_inc(s_hTb, 1)

            def weighted(i):
                h, u = i % 3, i % AHEAD
                e = expert_of(dve, i)
                dve.wait_ge(s_ye, i + 1)
                dve.tensor_tensor(yb[:, h, :], bank[4 + i % 2][:, 0:D], b2_sb[:, bass.ds(e, 1), :].rearrange("p a d -> p (a d)"),
                                  ALU.add).then_inc(s_yb, 1)
                dve.wait_ge(s_yb, i + 1)
                if i >= AHEAD:
                    dve.wait_ge(s_out[u], (i // AHEAD) * 16)
                dve.tensor_scalar(yw[:, u, :], yb[:, h, :], xg[:, u, D:D + 1], None, ALU.mult).then_inc(s_yw, 1)

            def dve_step(i):
                if i + 1 < SLOTS:
                    hidden_upper(i + 1)
                weighted(i)

            dve.wait_ge(s_w2, 32)
            hidden_upper(0)
            for i in range(SLOTS):
                dve_step(i)

            def shift(g):
                t = slice(g * FT, (g + 1) * FT)
                dve.wait_ge(s_frs, g + 1)
                dve.scalar_tensor_tensor(fshift[:, t], fmv[:, t, 0], -1.0, frstd[:, t], ALU.mult, ALU.mult).then_inc(s_fshift, 1)

            for g in range(T // FT):
                t = slice(g * FT, (g + 1) * FT)
                dve.wait_ge(s_acc0, g + 1)
                dve.tensor_tensor(acc[:, t, :], acc[:, t, :], ysum[:, t, D:2 * D], ALU.add).then_inc(s_acc, 1)
                dve.wait_ge(s_acc, g + 1)
                for n in range(g * FT, (g + 1) * FT):
                    dve.bn_stats(fstats[:, n, :], acc[:, n, :]).then_inc(s_fst, 1)
                for n in range(g * FT, (g + 1) * FT):
                    dve.wait_ge(s_fst, n + 1)
                    dve.bn_aggr(fmv[:, n, :], fstats[:, n, :]).then_inc(s_fmv, 1)
                if g:
                    shift(g - 1)
            shift(T // FT - 1)

        @block.tensor
        def _(pe):
            mm = nc.tensor.matmul

            def job(kind, g):
                i = at[kind, g]
                if i >= 8:
                    pe.wait_ge(*emptied(i - 8))
                b = bank[i % 8]
                c = slice(g * GROUP, (g + 1) * GROUP)
                if kind == "xT":
                    pe.wait_ge(s_x[g], 16)
                    if g == 0:
                        pe.wait_ge(s_const, 1)
                    for u in range(TG):
                        last = nc.tensor.transpose(b[:, u * P:(u + 1) * P], x_sb[:, g * TG + u, :], ident[:, :])
                elif kind == "wgk1T":
                    pe.wait_ge(s_gatew, 48)
                    last = nc.tensor.transpose(b[0:R, 0:P], wgk1_sb[:, :], ident[:, :])
                elif kind == "b1T":
                    pe.wait_ge(s_b1, 16)
                    last = nc.tensor.transpose(b[:, 0:E * HC], b1_in[:, :], ident[0:E * HC, 0:E * HC])
                elif kind == "span":
                    pe.wait_ge(s_widest, 1)
                    last = nc.tensor.transpose(b[0:1, 0:P], widest[:, :], ident[:, :])
                elif kind == "wgk":
                    pe.wait_ge(*emptied(at["wgk1T", 0]))
                    last = mm(b[:, 0:P], wgk1T[:, :], wgk2_sb[:, :], start=True, stop=True)
                elif kind == "z":
                    pe.wait_ge(*emptied(at["xT", g]))
                    pe.wait_ge(*emptied(at["wgk", 0]))
                    last = mm(b[:, :], wgk[:, :], xT[:, c], start=True, stop=True)
                elif kind in ("q", "k"):
                    if g == 0:
                        pe.wait_ge(s_projw, 32)
                    last = mm(b[:, :], (wq_sb if kind == "q" else wk_sb)[:, :], xT[:, c], start=True, stop=True)
                elif kind == "v":
                    if g == 0:
                        pe.wait_ge(s_vgw, 32)
                    for u in range(2):
                        t = 2 * g + u
                        last = mm(b[:, u * DV:(u + 1) * DV], xT[:, t * P:(t + 1) * P], wv_sb[:, :], start=True, stop=True)
                else:
                    m, n = g % DVC, g // DVC
                    last = mm(b[:, :], wg_sb[:, m * P:(m + 1) * P], xT[:, n * GROUP:(n + 1) * GROUP], start=True, stop=True)
                last.then_inc(s_job, 1)

            for kind, g, _ in jobs:
                job(kind, g)
            pe.wait_ge(s_jact, n_act)
            pe.wait_ge(s_jdve, n_dve)

            pe.wait_ge(s_flag, 1)
            too_wide = pe.value_load(wide_flag[0:1, 0:1], min_val=0, max_val=1)
            with pe.If(too_wide):
                with pe.Fori(0, dv) as v:
                    turn = v * V_STEPS + 1
                    pe.wait_ge(s_turn, turn + 1)
                    for t in range(T):
                        last = mm(bank[t // TG][:, (t % TG) * P:(t % TG + 1) * P],
                                  v_col[:, t, :, :].rearrange("p h k -> p (h k)"), ident[:, :], start=True, stop=True)
                    last.then_inc(s_turn, 1)
                    pe.wait_ge(s_turn, turn + 3 + 2 * NG)
                    for t in range(T):
                        last = mm(bank[4][:, t * HEADS:(t + 1) * HEADS], q_states[:, t * P:(t + 1) * P], head_pick[:, :],
                                  start=True, stop=True)
                    last.then_inc(s_turn, 1)
                pe.wait_ge(s_turn, V_END + 8)

            def scores(t):
                g = t // TG
                c = slice(t * P, (t + 1) * P)
                if t % TG == 0:
                    pe.wait_ge(s_km, g + 1)
                    pe.wait_ge(s_qc, g + 1)
                    pe.wait_ge(s_kc, g + 1)
                if t:
                    pe.wait_ge(s_aT, t)
                for h in range(HEADS):
                    r = slice(h * dk, (h + 1) * dk)
                    last = mm(bank[h][:, 0:P], km[r, c], qm[r, c], start=True, stop=True)
                last.then_inc(s_a, 1)

            def act_bank_read(i):
                for s, age in ((s_kcT, 0), (s_lrms, AGE_GATE), (s_x1T, AGE_X1T)):
                    t = at_age(i, age)
                    if t is not None:
                        pe.wait_ge(s, t + 1)

            def dve_bank_read(i):
                for s, age, steps in ((s_state, AGE_O, HEADS), (s_res, AGE_OUT, 1), (s_score, AGE_ROUTE, 1)):
                    t = at_age(i, age)
                    if t is not None:
                        pe.wait_ge(s, steps * (t + 1))
                b = batch_at(i, AGE_PLACE)
                if b is not None:
                    pe.wait_ge(s_place0, b + 1)

            def transpose_kc(t):
                return nc.tensor.transpose(bank[6][:, 0:P], kc[:, t * P:(t + 1) * P], ident[:, :])

            def sum_squares(t):
                pe.wait_ge(s_sq, t + 1)
                return mm(bank[6][:, 256:512], block_ones[:, :], sq[:, t % 2, :, :].rearrange("p c t -> p (c t)"),
                          start=True, stop=True)

            def transpose_x1(t):
                pe.wait_ge(s_x1, t + 1)
                return nc.tensor.transpose(bank[6][:, P:2 * P], xr[:, t, 0, 0:D], ident[:, :])

            def update(t):
                pe.wait_ge(s_kcT, t + 1)
                return mm(bank[7][:, 0:DV], kcT[:, t % 2, :], v_sb[:, t, :], start=True, stop=True)

            def project_out(t):
                pe.wait_ge(s_og, t + 1)
                for c in range(DVC):
                    last = mm(bank[7][:, 256:256 + D], ogT[:, t % 2, c, :], wo_sb[:, c, :], start=(c == 0), stop=(c == DVC - 1))
                return last

            def route(t):
                pe.wait_ge(s_x1T, t + 1)
                return mm(bank[7][:, 384:384 + E], x1T[:, t % 2, :], wr_sb[:, :], start=True, stop=True)

            def rank(b):
                pe.wait_ge(s_sofar, 2 * b + 2)
                mm(bank[7][:, 400:400 + 2 * E], before_count[:, :], hit[:, 2 * b:2 * b + 2, :].rearrange("p t e -> p (t e)"),
                   start=True, stop=False)
                return mm(bank[7][:, 400:400 + 2 * E], ones_count[:, :], so_far[:, 2 * b:2 * b + 2, :].rearrange("p t e -> p (t e)"),
                          start=False, stop=True)

            def attend(t):
                b = bank[4 + t % 2]
                pe.wait_ge(s_aT, t + 1)
                if t >= 2:
                    pe.wait_ge(s_og, t - 1)
                if t:
                    pe.wait_ge(s_state, HEADS * t)
                    for c in range(DVC):
                        mm(b[:, c * P:(c + 1) * P], state[:, (t - 1) % 2, c * P:(c + 1) * P], qc[:, t * P:(t + 1) * P],
                           start=(c == 0), stop=True, skip_group_check=True)
                for h in (0, 2, 1, 3):
                    c, r = h // DVC, (h % DVC) * dv
                    last = mm(b[r:r + dv, c * P:(c + 1) * P], v_sb[:, t, h * dv:(h + 1) * dv], aT[:, t % 2, h, :],
                              start=(t == 0 and c == 0), stop=True, skip_group_check=True)
                last.then_inc(s_o, 1)

            def write_act_bank(i):
                if i <= T - 1 + AGE_X1T:
                    if i:
                        act_bank_read(i - 1)
                    for age, stage in ((0, transpose_kc), (AGE_GATE, sum_squares), (AGE_X1T, transpose_x1)):
                        t = at_age(i, age)
                        if t is not None:
                            last = stage(t)
                    last.then_inc(s_act_bank, 1)

            def write_dve_bank(i):
                if i:
                    dve_bank_read(i - 1)
                    for age, stage in ((AGE_O, update), (AGE_OUT, project_out), (AGE_ROUTE, route)):
                        t = at_age(i, age)
                        if t is not None:
                            last = stage(t)
                    b = batch_at(i, AGE_PLACE)
                    if b is not None:
                        last = rank(b)
                    if i == ROUNDS - 1:
                        last = mm(bank[7][:, 432:432 + NB * E].rearrange("p (b e) -> p b e", e=E), ones_count[:, :],
                                  so_far[:, 2:T + 1:2, :], start=True, stop=True)
                    last.then_inc(s_dve_bank, 1)

            pe.wait_ge(s_wo2, 1)
            pe.wait_ge(s_router, 32)
            for i in range(ROUNDS):
                if i < T:
                    scores(i)
                for write in (write_act_bank, write_dve_bank) if i < T + 2 else (write_dve_bank, write_act_bank):
                    write(i)
                if at_age(i, AGE_O) is not None:
                    attend(i - AGE_O)

            pe.wait_ge(s_x1T, T)
            pe.wait_ge(s_tab, 3)
            mm(bank[6][:, 0:1], before[:, :], pair_used[:, :], start=True, stop=True).then_inc(s_pos, 1)
            pe.wait_ge(s_tab, 8)
            for k in range(3):
                last = mm(bank[6][0:1, 64 * (k + 1):64 * (k + 1) + SLOTS], pair_value[:, k:k + 1], in_slot[:, :],
                          start=True, stop=True)
            last.then_inc(s_entries, 1)
            pe.wait_ge(s_table, 3)
            pe.wait_ge(s_w2, 32)

            def transpose_rows(i):
                u = i % AHEAD
                pe.wait_ge(s_xg[u], (i // AHEAD + 1) * 16)
                if i:
                    pe.wait_ge(s_gT, i)
                nc.tensor.transpose(bank[7][:, 0:P], xg[:, u, 0:D], ident[:, :]).then_inc(s_gt, 1)

            def hidden(i):
                h, u = i % 3, i % AHEAD
                pe.wait_ge(s_gT, i + 1)
                pe.wait_ge(s_w1[u], (i // AHEAD + 1) * 16)
                if i >= 2:
                    pe.wait_ge(s_hTa, (i - 1) * (HC // 2))
                    pe.wait_ge(s_hTb, (i - 1) * (HC // 2))
                for half, s in ((0, s_ha), (1, s_hb)):
                    for k in range(HC // 2):
                        n = half * (HC // 2) + k
                        last = mm(bank[2 * (i % 2) + half][:, k * P:(k + 1) * P], w1_buf[u][:, n * P:(n + 1) * P], xgT[:, h, :],
                                  start=True, stop=True)
                    last.then_inc(s, 1)

            def expert_out(i, e):
                h = i % 3
                pe.wait_ge(s_hTa, (i + 1) * (HC // 2))
                pe.wait_ge(s_hTb, (i + 1) * (HC // 2))
                if i >= 2:
                    pe.wait_ge(s_yb, i - 1)
                w2_all = w2_sb[:, :, :].rearrange("p e c -> p (e c)")
                first = pe.snap(e * (HC * D))
                for n in range(HC):
                    last = mm(bank[4 + i % 2][:, 0:D], hT[:, h, n, :], w2_all[:, bass.ds(first + n * D, D)],
                              start=(n == 0), stop=(n == HC - 1))
                last.then_inc(s_ye, 1)

            def pe_step(i):
                if i + 1 < SLOTS:
                    hidden(i + 1)
                if i + 2 < SLOTS:
                    transpose_rows(i + 2)
                expert_out(i, expert_of(pe, i))

            transpose_rows(0)
            transpose_rows(1)
            hidden(0)
            for i in range(SLOTS):
                pe_step(i)

_INS = ['L0_attn_x', 'L0_attn_Wq', 'L0_attn_Wk', 'L0_attn_Wv', 'L0_attn_Wg', 'L0_attn_Wgk1', 'L0_attn_Wgk2', 'L0_attn_bgk2', 'L0_attn_Wo', 'L0_attn_g_norm_weight', 'L0_ffn_Wr', 'L0_ffn_br', 'L0_ffn_W1', 'L0_ffn_b1', 'L0_ffn_W2', 'L0_ffn_b2']
_OUTS = [((1, 2048, 128), 'float32')]


def kernel(**inputs):
    import numpy as _np
    import concourse.bacc as _bacc
    from concourse import mybir as _mybir
    from concourse.bass_utils import run_bass_kernel_spmd as _run

    nc = _bacc.Bacc("TRN2", target_bir_lowering=False, num_devices=1)
    arrays, args = {}, []
    for name in _INS:
        a = _np.ascontiguousarray(inputs[name])
        arrays[f"in_{name}_dram"] = a
        args.append(nc.dram_tensor(f"in_{name}_dram", a.shape, _mybir.dt.from_np(a.dtype), kind="ExternalInput").ap())
    for i, (shape, dtype) in enumerate(_OUTS):
        dt = _mybir.dt.from_np(_np.dtype(dtype))
        args.append(nc.dram_tensor(f"out_{i}_dram", shape, dt, kind="ExternalOutput").ap())
    build(nc, *args)
    r = _run(nc, [arrays], core_ids=[0])
    got = tuple(r.results[0][f"out_{i}_dram"] for i in range(len(_OUTS)))
    return got[0]
```
